# Optimizing a Trainium2 kernel written in Bass

```python
import numpy as np
import jax
import jax.numpy as jnp

def _softmax(x, axis=-1):
    return jax.nn.softmax(x, axis=axis)

def _gelu(x):
    return jax.nn.gelu(x, approximate=True)

def _silu(x):
    return jax.nn.silu(x)

def _sigmoid(x):
    return jax.nn.sigmoid(x)

def _layernorm(x, axis=-1, eps=1e-05):
    m = jnp.mean(x, axis=axis, keepdims=True)
    v = jnp.var(x, axis=axis, keepdims=True)
    return (x - m) / jnp.sqrt(v + eps)

def _scatter_add(tgt, idx, src, axis=0):
    return tgt.at[idx].add(src)

def _segment_sum(src, seg, n):
    return jax.ops.segment_sum(src, seg, n)
kernel_name = 'mk_seq_preln_d1_jaxref_r8_93c2b7'

def setup_inputs(seed: int=0):
    np.random.seed(seed)
    _w = jnp.asarray

    def _L0_attn_setup():
        import jax, jax.numpy as jnp
        import numpy as np
        B, T, D = (2, 256, 128)
        H, DH = (16, 64)
        BASE = 10000.0

        def _rotate_half(u):
            u1, u2 = (u[..., :u.shape[-1] // 2], u[..., u.shape[-1] // 2:])
            return jnp.concatenate((-u2, u1), axis=-1)

        def _rope_cos_sin(seq_len, dim, dtype):
            inv_freq = 1.0 / BASE ** (jnp.arange(0, dim, 2, dtype=jnp.float32) / dim)
            t = jnp.arange(seq_len, dtype=jnp.float32)
            freqs = jnp.einsum('i,j->ij', t, inv_freq)
            emb = jnp.concatenate((freqs, freqs), axis=-1)
            return (emb.astype(dtype), jnp.cos(emb).astype(dtype), jnp.sin(emb).astype(dtype))
        key = jax.random.key(seed)
        k1, k2, k3 = jax.random.split(key, 3)
        x = jax.random.normal(k1, (B, T, D), dtype=jnp.float32)
        qkv_w = jax.random.normal(k2, (3 * H * DH, D), dtype=jnp.float32) * np.sqrt(2.0 / (3 * H * DH))
        out_w = jax.random.normal(k3, (D, H * DH), dtype=jnp.float32) * np.sqrt(2.0 / D)
        return {'x': x, 'qkv_w': qkv_w, 'out_w': out_w}
    _L0_attn_in = _L0_attn_setup()

    def _L0_ffn_setup():
        import jax, jax.numpy as jnp
        import numpy as np
        CAPACITY_FACTOR = 1.25
        key = jax.random.key(seed)
        ks = jax.random.split(key, 6)
        B, S, H, E = (4, 512, 128, 8)
        scale = 1.0 / np.sqrt(H)
        return {'tokens': jax.random.normal(ks[0], (B, S, H), dtype=jnp.float32), 'gate_w': jax.random.normal(ks[1], (E, H), dtype=jnp.float32) * scale, 'w1': jax.random.normal(ks[2], (E, H, H), dtype=jnp.float32) * scale, 'b1': jax.random.normal(ks[3], (E, H), dtype=jnp.float32) * 0.01, 'w2': jax.random.normal(ks[4], (E, H, H), dtype=jnp.float32) * scale, 'b2': jax.random.normal(ks[5], (E, H), dtype=jnp.float32) * 0.01}
    _L0_ffn_in = _L0_ffn_setup()
    _d = {'L0_attn_x': _L0_attn_in['x'], 'L0_attn_qkv_w': _L0_attn_in['qkv_w'], 'L0_attn_out_w': _L0_attn_in['out_w'], 'L0_ffn_gate_w': _L0_ffn_in['gate_w'], 'L0_ffn_w1': _L0_ffn_in['w1'], 'L0_ffn_b1': _L0_ffn_in['b1'], 'L0_ffn_w2': _L0_ffn_in['w2'], 'L0_ffn_b2': _L0_ffn_in['b2']}
    _x0 = _d['L0_attn_x']
    _d['L0_attn_x'] = jax.random.normal(jax.random.fold_in(jax.random.key(seed), 1), (2, 1024, 128), dtype=_x0.dtype)
    del _x0
    return _d

def reference(L0_attn_x, L0_attn_qkv_w, L0_attn_out_w, L0_ffn_gate_w, L0_ffn_w1, L0_ffn_b1, L0_ffn_w2, L0_ffn_b2):

    def _L0_attn_ref(x, qkv_w, out_w):
        import jax, jax.numpy as jnp
        import numpy as np
        B, T, D = (2, 256, 128)
        H, DH = (16, 64)
        BASE = 10000.0

        def _rotate_half(u):
            u1, u2 = (u[..., :u.shape[-1] // 2], u[..., u.shape[-1] // 2:])
            return jnp.concatenate((-u2, u1), axis=-1)

        def _rope_cos_sin(seq_len, dim, dtype):
            inv_freq = 1.0 / BASE ** (jnp.arange(0, dim, 2, dtype=jnp.float32) / dim)
            t = jnp.arange(seq_len, dtype=jnp.float32)
            freqs = jnp.einsum('i,j->ij', t, inv_freq)
            emb = jnp.concatenate((freqs, freqs), axis=-1)
            return (emb.astype(dtype), jnp.cos(emb).astype(dtype), jnp.sin(emb).astype(dtype))
        b, t, d = x.shape
        qkv = jnp.einsum('btd,ed->bte', x, qkv_w)
        q, k, v = jnp.split(qkv, 3, axis=-1)

        def to_heads(u):
            return u.reshape(b, t, H, DH).transpose(0, 2, 1, 3)
        q, k, v = (to_heads(q), to_heads(k), to_heads(v))
        _, cos, sin = _rope_cos_sin(t, DH, x.dtype)
        cos = cos[None, None]
        sin = sin[None, None]
        q = q * cos + _rotate_half(q) * sin
        k = k * cos + _rotate_half(k) * sin
        scale = DH ** (-0.5)
        scores = jnp.einsum('bhqd,bhkd->bhqk', q, k) * scale
        causal = jnp.tril(jnp.ones((t, t), dtype=bool))
        scores = jnp.where(causal[None, None], scores, -jnp.inf)
        attn = jax.nn.softmax(scores, axis=-1)
        out = jnp.einsum('bhqk,bhkd->bhqd', attn, v)
        out = out.transpose(0, 2, 1, 3).reshape(b, t, H * DH)
        return jnp.einsum('bte,de->btd', out, out_w)

    def _L0_ffn_ref(tokens, gate_w, w1, b1, w2, b2):
        import jax, jax.numpy as jnp
        import numpy as np
        CAPACITY_FACTOR = 1.25
        B, S, H = tokens.shape
        E = gate_w.shape[0]
        N = B * S
        cap = int(CAPACITY_FACTOR * N / E)
        x = tokens.reshape(N, H)
        probs = jax.nn.softmax(x @ gate_w.T, axis=-1)
        top2_w, top2_idx = jax.lax.top_k(probs, 2)
        a_e = top2_idx.reshape(-1)
        a_w = top2_w.reshape(-1)
        tok_id = jnp.arange(2 * N) // 2
        counts = jnp.bincount(a_e, length=E)
        keep = counts <= cap
        valid = keep[a_e]
        onehot = jax.nn.one_hot(a_e, E, dtype=jnp.int32)
        pos = jnp.take_along_axis(jnp.cumsum(onehot, axis=0) - 1, a_e[:, None], axis=1)[:, 0]
        p = jnp.where(valid, jnp.minimum(pos, cap - 1), cap)
        x_a = x[tok_id]
        buf = jnp.zeros((E, cap + 1, H), dtype=x.dtype).at[a_e, p].set(x_a)
        h = jax.nn.silu(jnp.einsum('ech,efh->ecf', buf, w1) + b1[:, None, :])
        y = jnp.einsum('ecf,egf->ecg', h, w2) + b2[:, None, :]
        contrib = y[a_e, p] * (a_w * valid.astype(x.dtype))[:, None]
        out = contrib.reshape(N, 2, H).sum(axis=1)
        return out.reshape(B, S, H)
    x = L0_attn_x
    x = x + _L0_attn_ref(_layernorm(x, axis=-1), L0_attn_qkv_w, L0_attn_out_w)
    x = x + _L0_ffn_ref(_layernorm(x, axis=-1), L0_ffn_gate_w, L0_ffn_w1, L0_ffn_b1, L0_ffn_w2, L0_ffn_b2)
    return x

_drawn_inputs = setup_inputs


def setup_inputs(seed=0):
    import zlib

    import numpy as np

    out = dict(_drawn_inputs(seed))
    spreads = {}
    factors = {}
    for name, (base, spread) in spreads.items():
        noise = np.random.default_rng([zlib.crc32(name.encode()), seed]).standard_normal(out[name].shape)
        drawn = base * np.exp(spread * noise) if base else spread * noise
        out[name] = jnp.asarray(drawn.astype(out[name].dtype))
    for name, factor in factors.items():
        out[name] = (out[name] * factor).astype(out[name].dtype)
    return out
```

```python
from contextlib import ExitStack

import concourse.bass as bass
from concourse import mybir

F32 = mybir.dt.float32
F32R = mybir.dt.float32r
BF16 = mybir.dt.bfloat16
I32 = mybir.dt.int32
ALU = mybir.AluOpType
ACT = mybir.ActivationFunctionType
AX = mybir.AxisListType

P = 128
MASKED = -3.0e38
EPS = 1e-5

UNITS = [(0, 0), (0, 1), (1, 0), (1, 1)]
KT = [4, 8, 4, 8]
T_OF = [0, 4, 12, 16]
T_STEP = 24
S_STEP = 16
X_STEP = 8
J_STEP = 8


def step_order():
    events = [(u, ki) for u in range(4) for ki in range(KT[u])]
    extra = {
        (0, 3): [("Y", 1, 3)], (1, 0): [("J", 0)], (1, 1): [("J", 1)], (1, 2): [("J", 2)],
        (1, 3): [("J", 3), ("Y", 0, 0)], (1, 4): [("J", 4)], (1, 5): [("J", 5)], (1, 6): [("J", 6)],
        (1, 7): [("J", 7)], (2, 0): [], (2, 1): [("V",)], (2, 2): [("X", 0)], (2, 3): [("Y", 0, 1), ("X", 1)],
        (3, 0): [("X", 2)], (3, 1): [("X", 3)], (3, 2): [], (3, 3): [("Y", 0, 2)],
        (3, 4): [("X", 4)], (3, 5): [("X", 5)], (3, 6): [("X", 6)], (3, 7): [("X", 7)],
    }
    order = []
    for n, (u, ki) in enumerate(events):
        order.append(("T", u, ki))
        order.append(("PV", 1 if n < 2 else 0, *events[n - 2]))
        every = KT[u] // 4
        if ki % every == every - 1:
            order.append(("S", 1 if u == 3 else 0, (u + 1) % 4, ki // every))
        order += extra.get((u, ki), [])
    return order


ORDER = step_order()
SHARED = [i for i in ORDER if i[0] in ("J", "X", "Y")]


def attention_moe_kernel(nc, x, qkv_wT, out_wT, gate_wT, w1T, b1T, w2T, b2, cos, sin, ident_in, mask_in, lower_in, out):
    N, D = x.shape
    TILES = N // P
    B = 2
    QT = TILES // B
    E = gate_wT.shape[1]
    CAP = int(1.25 * N / E)
    PAIRS = qkv_wT.shape[1] // 384
    HEADS = 2 * PAIRS
    STEPS = 2 * PAIRS

    x_v = x.rearrange("(t p) d -> p t d", p=P)
    out_v = out.rearrange("(t p) d -> p t d", p=P)

    with ExitStack() as ctx:
        def sb(name, shape, dt=F32):
            return ctx.enter_context(nc.sbuf_tensor(name, shape, dt))

        def ps(name, shape, dt=F32):
            return ctx.enter_context(nc.psum_tensor(name, shape, dt))

        def sem(name):
            return ctx.enter_context(nc.semaphore(name))

        y = sb("y", [P, TILES, D])
        w_qkv = sb("w_qkv", [P, PAIRS * 384])
        w_out = sb("w_out", [P, HEADS, D])
        w_gate = sb("w_gate", [P, E])
        cos_s = sb("cos_s", [P, QT, 64])
        sin_s = sb("sin_s", [P, QT, 64])
        ident = sb("ident", [P, P])
        mask_f = sb("mask_f", [P, P])
        mask = sb("mask", [P, P], BF16)
        ident_b = sb("ident_b", [P, P], BF16)
        lower = sb("lower", [P, E, E])
        ones = sb("ones", [P, P])
        stats = sb("stats", [P, TILES, 6])
        mean_var = sb("mean_var", [P, TILES, 2])
        ve = sb("ve", [P, TILES])
        sd = sb("sd", [P, TILES])
        r0 = sb("r0", [P, TILES])
        r1 = sb("r1", [P, TILES])
        rstd = sb("rstd", [P, TILES])
        xnT = sb("xnT", [P, N])
        qkv = sb("qkv", [P, QT, 384])
        roped = sb("roped", [P, QT, 4, 2, 64])
        rope_cos = sb("rope_cos", [P, 4, 256])
        rope_sin = sb("rope_sin", [P, 4, 256])
        q_st = sb("q_st", [P, 2, 2, 1024], F32R)
        k_hi = sb("k_hi", [P, 2, 2, 1024], F32R)
        k_lo = sb("k_lo", [P, 2, 2, 1024], F32R)
        v_st = sb("v_st", [P, 2, QT, 2, P], F32R)
        p0 = sb("p0", [P, 1280])
        p1 = sb("p1", [P, 3328])
        pt_hi0 = sb("pt_hi0", [P, 1408], F32R)
        pt_lo0 = sb("pt_lo0", [P, 1408], F32R)
        pt_hi1 = sb("pt_hi1", [P, 3456], F32R)
        pt_lo1 = sb("pt_lo1", [P, 3456], F32R)
        neg_max = sb("neg_max", [P, S_STEP])
        row_sum = sb("row_sum", [P, 4, 4])
        inv_sum = sb("inv_sum", [P, 4, 4])
        o_t = sb("o_t", [P, 2, 512])
        xn = roped[:, 0:4, :, :, :].rearrange("p t a b d -> p (t a) (b d)")

        s_ps = ps("s_ps", [P, 2, 1024])
        pt_ps = ps("pt_ps", [P, 2, 512])
        o_ps = ps("o_ps", [P, 512])
        m_ps = ps("m_ps", [P, 512])

        load_x = sem("load_x")
        load_c = sem("load_c")
        load_w = sem("load_w")
        load_o = sem("load_o")
        const_ready = sem("const_ready")
        ln_step = sem("ln_step")
        sd_ready = sem("sd_ready")
        xn_ready = sem("xn_ready")
        xn_turned = sem("xn_turned")
        xnT_ready = sem("xnT_ready")
        proj_done = sem("proj_done")
        qkv_ready = sem("qkv_ready")
        rope_part = sem("rope_part")
        rope_ready = sem("rope_ready")
        turned = sem("turned")
        qk_hi_ready = sem("qk_hi_ready")
        qk_ready = sem("qk_ready")
        v_hi_ready = sem("v_hi_ready")
        v_ready = sem("v_ready")
        scores_ready = sem("scores_ready")
        max_ready = sem("max_ready")
        probs_ready = sem("probs_ready")
        pt_ready = sem("pt_ready")
        pt_hi_ready = sem("pt_hi_ready")
        pt_split = sem("pt_split")
        pv_done = sem("pv_done")
        o_ready = sem("o_ready")
        y_done = sem("y_done")
        inv_ready = sem("inv_ready")
        y_added = sem("y_added")
        gate_done = sem("gate_done")
        gate_step = sem("gate_step")
        gate_exp = sem("gate_exp")
        gate_shift = sem("gate_shift")
        count_part = sem("count_part")
        count_done = sem("count_done")
        flag_ready = sem("flag_ready")
        stored = sem("stored")
        fw_load = sem("fw_load")
        f_h = sem("f_h")
        f_z = sem("f_z")
        f_e = sem("f_e")
        f_act = sem("f_act")
        f_step = sem("f_step")
        f_y = sem("f_y")
        f_we = sem("f_we")
        f_add = sem("f_add")
        f_end = sem("f_end")

        lg = p0[:, 0:128].rearrange("p (t e) -> p t e", e=E)
        ex = p0[:, 128:256].rearrange("p (t e) -> p t e", e=E)
        pr = p0[:, 256:384].rearrange("p (t e) -> p t e", e=E)
        sel = p0[:, 384:512].rearrange("p (t e) -> p t e", e=E)
        wt = p0[:, 512:640].rearrange("p (t e) -> p t e", e=E)
        g_max = p0[:, 640:656]
        g_sum = p0[:, 656:672]
        g_inv = p0[:, 672:688]
        cnt = p0[:, 688:696]
        keep = p0[:, 696:704]
        any_kept = p0[:, 704:705]
        we = p0[:, 720:736]
        b1c = p0[:, 740:741]
        b2r = p0[0:1, 768:896]
        gt = p1[:, 0:1024].rearrange("p (t e j) -> p t e j", e=E, j=E)
        eq = p1[:, 1024:2048].rearrange("p (t e j) -> p t e j", e=E, j=E)
        z_s = p1[:, 2048:2560]
        e_s = p1[:, 2560:3072]
        w1_s = qkv[:, 0, 0:128]
        w2_s = qkv[:, 0, 128:256]
        hs = o_t[:, 0, :]
        flag = sb("flag", [P, 1], I32)

        def p_off(c, j):
            return sum((4 * c + i + 1) * P for i in range(j))

        def pt_cols(c, ki):
            start = 0
            for k in range(ki + 1):
                first = max(0, k - 4 * c)
                pad = 1 if first == 3 else 0
                width = (4 - first + pad) * P
                if k == ki:
                    return start, width, (first - pad) * P, pad * P
                start += width

        probs = [p0, p1]
        pt_hi = [pt_hi0, pt_hi1]
        pt_lo = [pt_lo0, pt_lo1]
        block = ctx.enter_context(nc.Block())

        def at(per_step, p, b, i):
            return p * (2 * per_step) + (b * per_step + i)

        def run(eng, step):
            for b in range(B):
                step(0, b, b == 0, False)
            with eng.Fori(1, PAIRS - 1) as p:
                for b in range(B):
                    step(p, b, False, False)
            for b in range(B):
                step(PAIRS - 1, b, False, b == 1)

        def skipped(item, first, last):
            back = item[0] in ("PV", "Y") and item[1] == 1
            ahead = item[0] in ("J", "X", "V") or (item[0] == "S" and item[1] == 1)
            return (first and back) or (last and ahead)

        @block.sync
        def _(sp):
            sp.dma_start(y[:, 0:QT, :], x_v[:, 0:QT, :]).then_inc(load_x, 16)
            sp.dma_start(y[:, QT:TILES, :], x_v[:, QT:TILES, :]).then_inc(load_x, 16)
            sp.dma_start(ident[:, :], ident_in).then_inc(load_c, 16)
            sp.dma_start(w_qkv[:, :], qkv_wT).then_inc(load_w, 16)
            sp.dma_start(cos_s[:, :, :], cos).then_inc(load_c, 16)
            sp.dma_start(sin_s[:, :, :], sin).then_inc(load_c, 16)
            sp.dma_start(mask_f[:, :], mask_in).then_inc(load_c, 16)
            sp.dma_start(lower[:, :, :], lower_in).then_inc(load_c, 16)
            sp.dma_start(w_out[0:64, :, :], out_wT).then_inc(load_o, 16)
            sp.dma_start(w_out[64:128, :, :], out_wT).then_inc(load_o, 16)
            sp.dma_start(w_gate[:, :], gate_wT).then_inc(load_o, 16)
            sp.wait_ge(y_added, 4 * STEPS)
            sp.dma_start(out_v, y[:, :, :]).then_inc(stored, 16)
            sp.wait_ge(stored, 16)
            sp.wait_ge(flag_ready, 1)
            kept = sp.value_load(flag[0:1, 0:1], min_val=0, max_val=1)
            with sp.If(kept):
                def load_expert(e):
                    sp.dma_start(w1_s, w1T[bass.ds(e, 1)].rearrange("a h f -> (a h) f")).then_inc(fw_load, 16)
                    sp.dma_start(w2_s, w2T[bass.ds(e, 1)].rearrange("a f g -> (a f) g")).then_inc(fw_load, 16)
                    sp.dma_start(b1c, b1T[bass.ds(e, 1)].rearrange("a f o -> (a f) o")).then_inc(fw_load, 16)
                    sp.dma_start(b2r, b2[bass.ds(e, 1)]).then_inc(fw_load, 16)

                load_expert(0)
                with sp.Fori(1, E) as e:
                    sp.wait_ge(f_add, e * 4)
                    load_expert(e)
                sp.wait_ge(f_add, 4 * E)
                sp.dma_start(out_v, y[:, :, :]).then_inc(stored, 16)
                sp.wait_ge(stored, 32)
            sp.nop()

        @block.gpsimd
        def _(pool):
            def rope(p, b, first):
                for hf in range(2):
                    t0 = 4 * hf
                    src = qkv[:, t0:t0 + 4, 0:256].rearrange("p t (s d) -> p t s d", d=64)
                    by_cos = rope_cos[:, :, :].rearrange("p t (s d) -> p t s d", d=64)
                    by_sin = rope_sin[:, :, :].rearrange("p t (s d) -> p t s d", d=64)

                    def table(tab, lo, n):
                        return tab[:, t0:t0 + 4, lo:lo + n].unsqueeze(2).to_broadcast([P, 4, 4, n])

                    def twice(a):
                        return a[:, :, :].rearrange("p t (s d) -> p (t s) d", d=64).unsqueeze(2).to_broadcast([P, 16, 2, 64])

                    pool.wait_ge(qkv_ready, at(J_STEP, p, b, 4 * hf + 4))
                    if first and hf == 0:
                        pool.wait_ge(load_c, 16 * 5)
                    else:
                        pool.wait_ge(rope_ready, at(2, p, b, hf))
                    pool.tensor_tensor(by_cos, src, table(cos_s, 0, 64), ALU.mult).then_inc(rope_part, 1)
                    pool.tensor_tensor(by_sin[:, :, :, 0:32], src[:, :, :, 32:64], table(sin_s, 0, 32),
                                       ALU.mult).then_inc(rope_part, 1)
                    pool.tensor_tensor(by_sin[:, :, :, 32:64], src[:, :, :, 0:32], table(sin_s, 32, 32),
                                       ALU.mult).then_inc(rope_part, 1)
                    pool.wait_ge(rope_part, at(6, p, b, 3 * hf + 3))
                    if first:
                        pool.wait_ge(xn_turned, 4)
                    else:
                        pool.wait_ge(turned, at(X_STEP, p, b - 1, 4 * hf + 4))
                    dst = roped[:, t0:t0 + 4, :, :, :].rearrange("p t s a d -> p (t s) a d")
                    pool.tensor_tensor(dst, twice(rope_cos), twice(rope_sin), ALU.add).then_inc(rope_ready, 1)

            for b in range(B):
                rope(0, b, b == 0)
            with pool.Fori(1, PAIRS) as p:
                for b in range(B):
                    rope(p, b, False)

        @block.scalar
        def _(act):
            def deviation(n):
                act.wait_ge(ln_step, n)
                nc.scalar.activation(sd[:, :], ve[:, :], ACT.Sqrt).then_inc(sd_ready, 1)

            def xn_copy(n0):
                for g in range(4):
                    act.wait_ge(xn_turned, n0 + g + 1)
                    nc.scalar.activation(xnT[:, 512 * g:512 * g + 512], pt_ps[:, g % 2, :],
                                         ACT.Copy).then_inc(xnT_ready, 1)

            def project(p, b, t, first):
                if t == 0 and not first:
                    act.wait_ge(rope_ready, at(2, p, b, 0))
                    act.wait_ge(v_ready, at(1, p, b, 0))
                act.wait_ge(proj_done, at(J_STEP, p, b, t + 1))
                nc.scalar.activation(qkv[:, t, :], m_ps[:, 0:384], ACT.Copy).then_inc(qkv_ready, 1)

            def high(p, b, xi, reused):
                hf, h, k = xi // 4, xi // 2 % 2, xi % 2
                if xi == 0 and reused:
                    act.wait_ge(scores_ready, at(S_STEP, p, b - 1, 0))
                act.wait_ge(turned, at(X_STEP, p, b, xi + 1))
                dst = (k_hi if k else q_st)[:, b % 2, h, 512 * hf:512 * hf + 512]
                nc.scalar.activation(dst, m_ps[:, :], ACT.Copy, scale=1.0 if k else 0.125).then_inc(qk_hi_ready, 1)

            def exps(p, b, u, j, early):
                c = UNITS[u][1]
                w = (4 * c + j + 1) * P
                if j == 0 and not early:
                    act.wait_ge(pt_ready, at(T_STEP, p, b, [-8, 0, 4, 12][u]))
                act.wait_ge(max_ready, at(S_STEP, p, b, 4 * u + j + 1))
                o = p_off(c, j)
                nc.scalar.activation(probs[c][:, o:o + w], s_ps[:, j % 2, 0:w], ACT.Exp,
                                     bias=neg_max[:, 4 * u + j:4 * u + j + 1],
                                     accum_out=row_sum[:, u, j:j + 1]).then_inc(probs_ready, 1)

            def step(p, b, first, last):
                start = first or (isinstance(p, int) and p == 0)
                pend = []
                for item in ORDER:
                    if skipped(item, first, last):
                        continue
                    if item[0] == "T":
                        _, u, ki = item
                        c = UNITS[u][1]
                        if ki == 0 and not (first and u < 2):
                            act.wait_ge(pv_done, at(4, p, b, u - 1))
                        act.wait_ge(pt_ready, at(T_STEP, p, b, T_OF[u] + ki + 1))
                        o, w, _, pad = pt_cols(c, ki)
                        nc.scalar.activation(pt_hi[c][:, o + pad:o + w], pt_ps[:, ki % 2, 0:w - pad],
                                             ACT.Copy).then_inc(pt_hi_ready, 1)
                    elif item[0] == "PV":
                        _, d, u, ki = item
                        if ki == KT[u] - 1:
                            if not (first and d == 0 and u < 2):
                                act.wait_ge(y_done, at(4, p, b - d, u - 1))
                            act.wait_ge(pv_done, at(4, p, b - d, u + 1))
                            nc.scalar.activation(o_t[:, u % 2, :], o_ps[:, :], ACT.Copy).then_inc(o_ready, 1)
                    elif item[0] == "S":
                        _, d, u, j = item
                        exps(p, b + d, u, j, first and d == 0 and u < 2)
                    elif item[0] == "J":
                        project(p, b + 1, item[1], False)
                    elif item[0] == "X":
                        high(p, b + 1, item[1], not first)

            deviation(1)
            xn_copy(0)
            for t in range(QT):
                project(0, 0, t, True)
            for xi in range(X_STEP):
                high(0, 0, xi, False)
            for j in range(4):
                exps(0, 0, 0, j, True)
            run(act, step)
            for ki in range(6, 8):
                pass
            act.wait_ge(y_done, 4 * STEPS - 2)
            act.wait_ge(pv_done, 4 * STEPS)
            nc.scalar.activation(o_t[:, 1, :], o_ps[:, :], ACT.Copy).then_inc(o_ready, 1)

            deviation(2)
            xn_copy(4)
            act.wait_ge(gate_shift, 1)
            nc.scalar.activation(ex, lg, ACT.Exp).then_inc(gate_exp, 1)

            act.wait_ge(flag_ready, 1)
            kept = act.value_load(flag[0:1, 0:1], min_val=0, max_val=1)
            with act.If(kept):
                with act.Fori(0, E) as e:
                    act.wait_ge(fw_load, e * 64 + 64)
                    for g in range(4):
                        act.wait_ge(f_h, e * 4 + (g + 1))
                        nc.scalar.activation(z_s, o_ps[:, :], ACT.Identity, bias=b1c).then_inc(f_z, 1)
                        act.wait_ge(f_z, e * 4 + (g + 1))
                        nc.scalar.activation(e_s, z_s, ACT.Exp, scale=-1.0).then_inc(f_e, 1)
            act.nop()

        @block.vector
        def _(dve):
            def layernorm(k):
                for t in range(TILES):
                    nc.vector.bn_stats(stats[:, t, :], y[:, t, :]).then_inc(gate_step, 1)
                dve.wait_ge(gate_step, link[0] + TILES)
                for t in range(TILES):
                    nc.vector.bn_aggr(mean_var[:, t, :], stats[:, t, :]).then_inc(gate_step, 1)
                dve.wait_ge(gate_step, link[0] + 2 * TILES)
                link[0] += 2 * TILES
                nc.vector.tensor_scalar(ve[:, :], mean_var[:, :, 1], EPS, None, ALU.add).then_inc(ln_step, 1)
                dve.wait_ge(sd_ready, k)
                after(nc.vector.reciprocal(r0[:, :], sd[:, :]))
                after(nc.vector.tensor_tensor(r1[:, :], r0[:, :], r0[:, :], ALU.mult))
                after(nc.vector.tensor_tensor(r1[:, :], r1[:, :], ve[:, :], ALU.mult))
                after(nc.vector.tensor_scalar(r1[:, :], r1[:, :], -0.5, 1.5, ALU.mult, ALU.add))
                after(nc.vector.tensor_tensor(rstd[:, :], r0[:, :], r1[:, :], ALU.mult))
                for t in range(TILES):
                    ins = nc.vector.tensor_scalar(xn[:, t, :], y[:, t, :], mean_var[:, t, 0:1], rstd[:, t:t + 1],
                                                  ALU.subtract, ALU.mult)
                    ins.then_inc(xn_ready, 1)

            link = [0]

            def after(ins):
                ins.then_inc(gate_step, 1)
                link[0] += 1
                dve.wait_ge(gate_step, link[0])

            def low(p, b, xi):
                hf, h, k = xi // 4, xi // 2 % 2, xi % 2
                cols = slice(512 * hf, 512 * hf + 512)
                dve.wait_ge(qk_hi_ready, at(X_STEP, p, b, xi + 1))
                if k:
                    nc.vector.tensor_tensor(k_lo[:, b % 2, h, cols], m_ps[:, :], k_hi[:, b % 2, h, cols],
                                            ALU.subtract).then_inc(qk_ready, 1)
                else:
                    q = q_st[64:128, b % 2, h, cols]
                    nc.vector.scalar_tensor_tensor(out=q, in0=m_ps[64:128, :], scalar=0.125, in1=q,
                                                   op0=ALU.mult, op1=ALU.subtract).then_inc(qk_ready, 1)

            def values(p, b, reused):
                v = qkv[:, :, 256:384].rearrange("p t (h d) -> p t h d", d=64)
                dve.wait_ge(qkv_ready, at(J_STEP, p, b, J_STEP))
                if reused:
                    dve.wait_ge(pv_done, at(4, p, b - 1, 0))
                dst = v_st[:, b % 2, :, :, :]
                nc.vector.tensor_copy(dst[:, :, :, 0:64], v).then_inc(v_hi_ready, 1)
                dve.wait_ge(v_hi_ready, at(1, p, b, 1))
                nc.vector.tensor_tensor(dst[:, :, :, 64:128], v, dst[:, :, :, 0:64], ALU.subtract).then_inc(v_ready, 1)

            def maxes(p, b, u, j):
                w = (4 * UNITS[u][1] + j + 1) * P
                dve.wait_ge(scores_ready, at(S_STEP, p, b, 4 * u + j + 1))
                nc.vector.tensor_reduce(neg_max[:, 4 * u + j:4 * u + j + 1], s_ps[:, j % 2, 0:w], AX.X, ALU.max,
                                        negate=True).then_inc(max_ready, 1)

            def add_y(p, b, u):
                c = UNITS[u][1]
                dve.wait_ge(probs_ready, at(S_STEP, p, b, 4 * u + 4))
                nc.vector.reciprocal(inv_sum[:, u, :], row_sum[:, u, :]).then_inc(inv_ready, 1)
                dve.wait_ge(inv_ready, at(4, p, b, u + 1))
                dve.wait_ge(y_done, at(4, p, b, u + 1))
                for j in range(4):
                    rows = y[:, QT * (b % 2) + 4 * c + j, :]
                    ins = nc.vector.scalar_tensor_tensor(out=rows, in0=m_ps[:, j * P:(j + 1) * P],
                                                         scalar=inv_sum[:, u, j:j + 1], in1=rows,
                                                         op0=ALU.mult, op1=ALU.add)
                ins.then_inc(y_added, 1)

            def step(p, b, first, last):
                for item in ORDER:
                    if skipped(item, first, last):
                        continue
                    if item[0] == "T":
                        _, u, ki = item
                        c = UNITS[u][1]
                        o, w, _, pad = pt_cols(c, ki)
                        dve.wait_ge(pt_hi_ready, at(T_STEP, p, b, T_OF[u] + ki + 1))
                        nc.vector.tensor_tensor(pt_lo[c][:, o + pad:o + w], pt_ps[:, ki % 2, 0:w - pad],
                                                pt_hi[c][:, o + pad:o + w], ALU.subtract).then_inc(pt_split, 1)
                    elif item[0] == "S":
                        maxes(p, b + item[1], item[2], item[3])
                    elif item[0] == "Y":
                        if not (first and item[1] == 0 and item[2] == 0):
                            dve.wait_ge(y_added, at(4, p, b - item[1], item[2]))
                        add_y(p, b - item[1], item[2])
                    elif item[0] == "V":
                        values(p, b + 1, not first)
                    elif item[0] == "X":
                        low(p, b + 1, item[1])

            nc.vector.memset(ones[:, :], 1.0).then_inc(const_ready, 1)
            for t in (pt_hi0, pt_lo0, pt_hi1, pt_lo1):
                n = t.shape[1]
                nc.vector.memset(t[:, n - 256:n - 128].bitcast(F32), 0.0).then_inc(const_ready, 1)
            dve.wait_ge(load_c, 16 * 5)
            nc.vector.tensor_copy(mask[:, :], mask_f[:, :]).then_inc(const_ready, 1)
            nc.vector.tensor_copy(ident_b[:, :], ident[:, :]).then_inc(const_ready, 1)
            dve.wait_ge(load_x, 32)
            layernorm(1)
            values(0, 0, False)
            for xi in range(X_STEP):
                low(0, 0, xi)
            for j in range(4):
                maxes(0, 0, 0, j)
            run(dve, step)
            dve.wait_ge(y_added, 4 * STEPS - 1)
            add_y(PAIRS - 1, 1, 3)

            dve.wait_ge(y_added, 4 * STEPS)
            layernorm(2)
            dve.wait_ge(gate_done, 1)
            logits = m_ps[:, 0:TILES * E].rearrange("p (t e) -> p t e", e=E)
            wide = [P, TILES, E]
            after(nc.vector.tensor_reduce(g_max, logits, AX.X, ALU.max))
            nc.vector.tensor_tensor(lg, logits, g_max.unsqueeze(2).to_broadcast(wide), ALU.subtract).then_inc(gate_shift, 1)
            dve.wait_ge(gate_exp, 1)
            after(nc.vector.tensor_reduce(g_sum, ex, AX.X, ALU.add))
            after(nc.vector.reciprocal(g_inv, g_sum))
            after(nc.vector.tensor_tensor(pr, ex, g_inv.unsqueeze(2).to_broadcast(wide), ALU.mult))
            other = pr.unsqueeze(2).to_broadcast([P, TILES, E, E])
            own = pr.unsqueeze(3).to_broadcast([P, TILES, E, E])
            nc.vector.tensor_tensor(gt, other, own, ALU.is_gt).then_inc(gate_step, 1)
            link[0] += 1
            after(nc.vector.tensor_tensor(eq, other, own, ALU.is_equal))
            after(nc.vector.tensor_tensor(eq, eq, lower[:, :, :].unsqueeze(1).to_broadcast([P, TILES, E, E]), ALU.mult))
            after(nc.vector.tensor_tensor(gt, gt, eq, ALU.add))
            after(nc.vector.tensor_reduce(sel, gt, AX.X, ALU.add))
            after(nc.vector.tensor_scalar(sel, sel, 2.0, None, ALU.is_lt))
            nc.vector.tensor_reduce(cnt, sel.rearrange("p t e -> p e t"), AX.X, ALU.add).then_inc(count_part, 1)
            dve.wait_ge(count_done, 1)
            after(nc.vector.tensor_scalar(keep, m_ps[:, 256:256 + E], float(CAP), None, ALU.is_le))
            after(nc.vector.tensor_reduce(any_kept, keep, AX.X, ALU.max))
            nc.vector.tensor_copy(flag[:, :], any_kept).then_inc(flag_ready, 1)
            dve.wait_ge(flag_ready, 1)
            kept = dve.value_load(flag[0:1, 0:1], min_val=0, max_val=1)
            with dve.If(kept):
                after(nc.vector.tensor_tensor(sel, sel, keep.unsqueeze(1).to_broadcast(wide), ALU.mult))
                after(nc.vector.tensor_tensor(wt, pr, sel, ALU.mult))
                with dve.Fori(0, E) as e:
                    nc.vector.tensor_copy(we.unsqueeze(2), wt[:, :, bass.ds(e, 1)]).then_inc(f_we, 1)
                    for g in range(4):
                        dve.wait_ge(f_e, e * 4 + (g + 1))
                        nc.vector.tensor_scalar(e_s, e_s, 1.0, None, ALU.add).then_inc(f_step, 1)
                        dve.wait_ge(f_step, e * 8 + (2 * g + 1))
                        nc.vector.reciprocal(e_s, e_s).then_inc(f_step, 1)
                        dve.wait_ge(f_step, e * 8 + (2 * g + 2))
                        nc.vector.tensor_tensor(hs, z_s, e_s, ALU.mult).then_inc(f_act, 1)
                        dve.wait_ge(f_we, e + 1)
                        dve.wait_ge(f_y, e * 4 + (g + 1))
                        for j in range(4):
                            rows = y[:, 4 * g + j, :]
                            ins = nc.vector.scalar_tensor_tensor(out=rows, in0=m_ps[:, j * P:(j + 1) * P],
                                                                 scalar=we[:, 4 * g + j:4 * g + j + 1], in1=rows,
                                                                 op0=ALU.mult, op1=ALU.add)
                        ins.then_inc(f_add, 1)
                        dve.wait_ge(f_add, e * 4 + (g + 1))
            dve.nop()

        @block.tensor
        def _(pe):
            def turn_xn(n0):
                for g in range(4):
                    pe.wait_ge(xn_ready, n0 + 4 * g + 4)
                    if g >= 2:
                        pe.wait_ge(xnT_ready, n0 // 4 + g - 1)
                    for t in range(4):
                        mm = nc.tensor.transpose(pt_ps[:, g % 2, t * P:(t + 1) * P], xn[:, 4 * g + t, :], ident[:, :])
                    mm.then_inc(xn_turned, 1)

            def shared_free(p, b, item):
                if item[0] == "J":
                    pe.wait_ge(qkv_ready, at(J_STEP, p, b, item[1] + 1))
                elif item[0] == "X":
                    pe.wait_ge(qk_ready, at(X_STEP, p, b, item[1] + 1))
                else:
                    pe.wait_ge(y_added, at(4, p, b, item[2] + 1))

            def project(p, b, t):
                w = w_qkv[:, bass.ds(p * 384, 384)] if b < 2 else w_qkv[:, bass.ds(p * 384 + 384, 384)]
                col = (QT * (b % 2) + t) * P
                nc.tensor.matmul(m_ps[:, 0:384], xnT[:, col:col + P], w, start=True, stop=True).then_inc(proj_done, 1)

            def turn(p, b, xi):
                hf, h, k = xi // 4, xi // 2 % 2, xi % 2
                pe.wait_ge(rope_ready, at(2, p, b, hf + 1))
                for t in range(4):
                    src = roped[:, 4 * hf + t, 2 * k + h, :, :].rearrange("p a d -> p (a d)")
                    mm = nc.tensor.transpose(m_ps[:, t * P:(t + 1) * P], src, ident[:, :])
                mm.then_inc(turned, 1)

            def scores(p, b, u, j, early):
                h, c = UNITS[u]
                qt = 4 * c + j
                width = (qt + 2) // 2 * 2 * P
                if not early:
                    pe.wait_ge(probs_ready, at(S_STEP, p, b, 4 * u + j - 1))
                if j == 0:
                    pe.wait_ge(qk_ready, at(X_STEP, p, b, [2, 6, 6, 8][u]))
                q = q_st[:, b % 2, h, qt * P:(qt + 1) * P]
                for lo in range(0, width, 512):
                    hi = min(lo + 512, width)
                    diag = lo <= qt * P < hi
                    o = s_ps[:, j % 2, lo:hi]
                    nc.tensor.matmul(o, q, k_hi[:, b % 2, h, lo:hi], start=True, stop=False)
                    mm = nc.tensor.matmul(o, q, k_lo[:, b % 2, h, lo:hi], start=False, stop=not diag)
                mm = nc.tensor.matmul(s_ps[:, j % 2, qt * P:(qt + 1) * P], ident_b[:, :], mask[:, :],
                                      start=False, stop=True)
                mm.then_inc(scores_ready, 1)

            def values(p, b, u, ki):
                h, c = UNITS[u]
                pe.wait_ge(pt_split, at(T_STEP, p, b, T_OF[u] + ki + 1))
                o, w, first_col, _ = pt_cols(c, ki)
                v = v_st[:, b % 2, ki, h, :]
                last = ki == KT[u] - 1
                nc.tensor.matmul(o_ps[:, first_col:512], v, pt_hi[c][:, o:o + w], start=(ki == 0), stop=False)
                mm = nc.tensor.matmul(o_ps[:, first_col:512], v, pt_lo[c][:, o:o + w], start=False, stop=last)
                if last:
                    mm.then_inc(pv_done, 1)

            def output(p, b, u):
                h = UNITS[u][0]
                pe.wait_ge(o_ready, at(4, p, b, u + 1))
                head = p * 2 + h if b >= 0 else p * 2 + (h - 2)
                w = w_out[:, bass.ds(head, 1), :].rearrange("p a d -> p (a d)")
                for j in range(4):
                    mm = nc.tensor.matmul(m_ps[:, j * P:(j + 1) * P], o_t[:, u % 2, j * P:(j + 1) * P], w,
                                          start=True, stop=True)
                mm.then_inc(y_done, 1)

            def step(p, b, first, last):
                before = (b, ("X", X_STEP - 1))
                for item in ORDER:
                    if skipped(item, first, last):
                        continue
                    if item[0] in ("J", "X", "Y"):
                        shared_free(p, *before)
                    if item[0] == "T":
                        _, u, ki = item
                        c = UNITS[u][1]
                        if ki == 0:
                            pe.wait_ge(probs_ready, at(S_STEP, p, b, 4 * u + 4))
                        if not (first and u == 0 and ki < 2):
                            pe.wait_ge(pt_split, at(T_STEP, p, b, T_OF[u] + ki - 1))
                        j0 = max(0, ki - 4 * c)
                        for j in range(j0, 4):
                            o = p_off(c, j) + ki * P
                            mm = nc.tensor.transpose(pt_ps[:, ki % 2, (j - j0) * P:(j - j0 + 1) * P],
                                                     probs[c][:, o:o + P], ident[:, :])
                        mm.then_inc(pt_ready, 1)
                    elif item[0] == "PV":
                        _, d, u, ki = item
                        if ki == 0:
                            if not (first and u == 0):
                                pe.wait_ge(o_ready, at(4, p, b, u))
                            if u == 0:
                                pe.wait_ge(v_ready, at(1, p, b, 1))
                        values(p, b - d, u, ki)
                    elif item[0] == "S":
                        scores(p, b + item[1], item[2], item[3], False)
                    elif item[0] == "J":
                        project(p, b + 1, item[1])
                        before = (b + 1, item)
                    elif item[0] == "X":
                        turn(p, b + 1, item[1])
                        before = (b + 1, item)
                    elif item[0] == "Y":
                        output(p, b - item[1], item[2])
                        before = (b - item[1], item)

            pe.wait_ge(load_c, 16 * 5)
            turn_xn(0)
            pe.wait_ge(xnT_ready, 4)
            pe.wait_ge(load_w, 16)
            pe.wait_ge(load_o, 48)
            pe.wait_ge(const_ready, 7)
            for t in range(QT):
                if t:
                    shared_free(0, 0, ("J", t - 1))
                project(0, 0, t)
            shared_free(0, 0, ("J", QT - 1))
            for xi in range(X_STEP):
                if xi:
                    shared_free(0, 0, ("X", xi - 1))
                turn(0, 0, xi)
            for j in range(4):
                scores(0, 0, 0, j, j < 2)
            run(pe, step)
            for ki in (6, 7):
                values(PAIRS - 1, 1, 3, ki)
            pe.wait_ge(y_added, 4 * STEPS - 1)
            output(PAIRS - 1, 1, 3)

            turn_xn(TILES)
            pe.wait_ge(y_added, 4 * STEPS)
            pe.wait_ge(xnT_ready, 8)
            for t in range(TILES):
                mm = nc.tensor.matmul(m_ps[:, t * E:(t + 1) * E], xnT[:, t * P:(t + 1) * P], w_gate[:, :],
                                      start=True, stop=True)
            mm.then_inc(gate_done, 1)
            pe.wait_ge(count_part, 1)
            nc.tensor.matmul(m_ps[:, 256:256 + E], ones[:, :], cnt, start=True, stop=True).then_inc(count_done, 1)

            pe.wait_ge(flag_ready, 1)
            kept = pe.value_load(flag[0:1, 0:1], min_val=0, max_val=1)
            with pe.If(kept):
                with pe.Fori(0, E) as e:
                    pe.wait_ge(fw_load, e * 64 + 64)
                    for g in range(4):
                        nc.tensor.matmul(o_ps[:, :], w1_s, xnT[:, 512 * g:512 * g + 512],
                                         start=True, stop=True).then_inc(f_h, 1)
                        pe.wait_ge(f_act, e * 4 + (g + 1))
                        for j in range(4):
                            o = m_ps[:, j * P:(j + 1) * P]
                            nc.tensor.matmul(o, hs[:, j * P:(j + 1) * P], w2_s, start=True, stop=False)
                            mm = nc.tensor.matmul(o, ones[0:1, :], b2r, start=False, stop=True)
                        mm.then_inc(f_y, 1)
                        pe.wait_ge(f_add, e * 4 + (g + 1))
            pe.nop()


def kernel(L0_attn_x, L0_attn_qkv_w, L0_attn_out_w, L0_ffn_gate_w, L0_ffn_w1, L0_ffn_b1, L0_ffn_w2, L0_ffn_b2):
    import numpy as np
    import concourse.bacc as bacc
    from concourse.bass_utils import run_bass_kernel_spmd

    f32 = np.float32
    nb, T, D = L0_attn_x.shape
    N = nb * T
    E = L0_ffn_gate_w.shape[0]
    HD = L0_attn_out_w.shape[1]
    DH = 64
    pairs = HD // 128
    c = np.ascontiguousarray

    inv_freq = (f32(1.0) / np.power(f32(10000.0), np.arange(0, DH, 2, dtype=f32) / f32(DH))).astype(f32)
    freqs = np.arange(T, dtype=f32)[:, None] * inv_freq[None, :]
    cosv, sinv = np.cos(freqs).astype(f32), np.sin(freqs).astype(f32)
    cos = np.concatenate([cosv, cosv], 1).reshape(T // 128, 128, DH).transpose(1, 0, 2)
    sin = np.concatenate([-sinv, sinv], 1).reshape(T // 128, 128, DH).transpose(1, 0, 2)

    arrays = {
        "x": c(np.asarray(L0_attn_x).reshape(N, D)),
        "qkv_wT": c(np.asarray(L0_attn_qkv_w).reshape(3, pairs, 128, D).transpose(3, 1, 0, 2).reshape(D, 3 * HD)),
        "out_wT": c(np.asarray(L0_attn_out_w).reshape(D, HD // DH, DH).transpose(2, 1, 0)),
        "gate_wT": c(np.asarray(L0_ffn_gate_w).T),
        "w1T": c(np.asarray(L0_ffn_w1).transpose(0, 2, 1)),
        "b1T": c(np.asarray(L0_ffn_b1).reshape(E, D, 1)),
        "w2T": c(np.asarray(L0_ffn_w2).transpose(0, 2, 1)),
        "b2": c(np.asarray(L0_ffn_b2)),
        "cos": c(cos),
        "sin": c(sin),
        "ident_in": np.eye(128, dtype=f32),
        "mask_in": np.triu(np.full((128, 128), MASKED, dtype=f32), 1),
        "lower_in": c(np.broadcast_to(np.tril(np.ones((E, E), dtype=f32), -1), (128, E, E))),
    }
    nc = bacc.Bacc("TRN2", target_bir_lowering=False, num_devices=1)
    args = [nc.dram_tensor(f"in_{k}", a.shape, mybir.dt.from_np(a.dtype), kind="ExternalInput").ap()
            for k, a in arrays.items()]
    out = nc.dram_tensor("out_y", (N, D), F32, kind="ExternalOutput").ap()
    attention_moe_kernel(nc, *args, out)
    r = run_bass_kernel_spmd(nc, [{f"in_{k}": a for k, a in arrays.items()}], core_ids=[0])
    return r.results[0]["out_y"].reshape(nb, T, D)
```

```python
from contextlib import ExitStack

import concourse.bass as bass
from concourse import mybir

F32 = mybir.dt.float32
F32R = mybir.dt.float32r
BF16 = mybir.dt.bfloat16
I32 = mybir.dt.int32
ALU = mybir.AluOpType
ACT = mybir.ActivationFunctionType
AX = mybir.AxisListType

P = 128
MASKED = -3.0e38
EPS = 1e-5

UNITS = [(0, 0), (0, 1), (1, 0), (1, 1)]
KT = [4, 8, 4, 8]
T_OF = [0, 4, 12, 16]
T_STEP = 24
LAG = 3
S_STEP = 16
SPREADS = 8
X_STEP = 4
J_STEP = 8


def step_order():
    events = [(u, ki) for u in range(4) for ki in range(KT[u])]
    extra = {
        (0, 0): [("J", 0)], (0, 1): [("J", 1)], (0, 2): [("J", 2)], (0, 3): [("Y", 1, 3), ("J", 3)],
        (1, 0): [("J", 4)], (1, 1): [("J", 5)], (1, 2): [("J", 6)], (1, 3): [("J", 7)],
        (1, 4): [("Y", 0, 0)], (1, 5): [("X", 0)], (1, 6): [("X", 1)],
        (2, 1): [("X", 2)], (2, 2): [("X", 3)], (2, 3): [("Y", 0, 1)],
        (3, 3): [("Y", 0, 2)],
    }
    order = []
    for n, (u, ki) in enumerate(events):
        order.append(("T", u, ki))
        order.append(("PV", 1 if n < LAG else 0, *events[n - LAG]))
        ahead = 1 if u == 3 else 0
        if UNITS[u][1] == 1:
            if ki < 4:
                order.append(("S", ahead, (u + 1) % 4, ki))
            if ki == 7:
                order.append(("S", ahead, (u + 2) % 4, 0))
        elif ki < 3:
            order.append(("S", 0, u + 1, ki + 1))
        order += extra.get((u, ki), [])
    return order


def exp_later(order):
    out = []
    held = [("S", 0, 1, 0)]
    for item in order:
        if item[0] == "S" and item[3] < 3:
            held.append(item)
            continue
        out.append(item)
        if item[0] == "T":
            out += held
            held = []
    return out


ORDER = step_order()
ACT_ORDER = exp_later(ORDER)
RING = 3
SHARED = [i for i in ORDER if i[0] in ("T", "J", "X", "Y")]
BANK = {item: n % RING for n, item in enumerate(SHARED)}


def bank_before(item, first, last):
    n, back = SHARED.index(item), 0
    while True:
        n -= 1
        if n < 0:
            if first:
                return None
            n, back = len(SHARED) - 1, 1
        was = SHARED[n]
        absent = (first and was[0] == "Y" and was[1] == 1) or (last and not back and was[0] in ("J", "X"))
        if BANK[was] == BANK[item] and not absent:
            return was, back


def attention_moe_kernel(nc, x, qkv_wT, out_wT, gate_wT, w1T, b1T, w2T, b2, cos, sin, ident_in, mask_in, lower_in, out):
    N, D = x.shape
    TILES = N // P
    B = 2
    QT = TILES // B
    E = gate_wT.shape[1]
    CAP = int(1.25 * N / E)
    PAIRS = qkv_wT.shape[1] // 384
    HEADS = 2 * PAIRS
    STEPS = 2 * PAIRS

    x_v = x.rearrange("(t p) d -> p t d", p=P)
    out_v = out.rearrange("(t p) d -> p t d", p=P)

    with ExitStack() as ctx:
        def sb(name, shape, dt=F32):
            return ctx.enter_context(nc.sbuf_tensor(name, shape, dt))

        def ps(name, shape, dt=F32):
            return ctx.enter_context(nc.psum_tensor(name, shape, dt))

        def sem(name):
            return ctx.enter_context(nc.semaphore(name))

        y = sb("y", [P, TILES, D])
        w_qkv = sb("w_qkv", [P, PAIRS * 384])
        w_out = sb("w_out", [P, HEADS, D])
        w_gate = sb("w_gate", [P, E])
        cos_s = sb("cos_s", [P, QT, 64])
        sin_s = sb("sin_s", [P, QT, 64])
        ident = sb("ident", [P, P])
        mask_f = sb("mask_f", [P, P])
        mask = sb("mask", [P, P], BF16)
        ident_b = sb("ident_b", [P, P], BF16)
        lower = sb("lower", [P, E, E])
        ones = sb("ones", [P, P])
        stats = sb("stats", [P, TILES, 6])
        mean_var = sb("mean_var", [P, TILES, 2])
        ve = sb("ve", [P, TILES])
        sd = sb("sd", [P, TILES])
        r0 = sb("r0", [P, TILES])
        r1 = sb("r1", [P, TILES])
        rstd = sb("rstd", [P, TILES])
        xnT = sb("xnT", [P, N])
        qkv = sb("qkv", [P, QT, 384])
        roped = sb("roped", [P, QT, 256])
        rope_sin = sb("rope_sin", [P, 4, 256])
        qk_pair = sb("qk_pair", [P, 2, 2, 2, 512], F32R)
        q_st = sb("q_st", [P, 2, 2, 1024], F32R)
        k_st = sb("k_st", [P, 2, 2, 2, 1024], F32R)
        v_st = sb("v_st", [P, 2, QT, 2, P], F32R)
        p0 = sb("p0", [P, 1280])
        p1 = sb("p1", [P, 3328])
        pt_hi0 = sb("pt_hi0", [P, 1408], F32R)
        pt_lo0 = sb("pt_lo0", [P, 1408], F32R)
        pt_hi1 = sb("pt_hi1", [P, 3456], F32R)
        pt_lo1 = sb("pt_lo1", [P, 3456], F32R)
        neg_max = sb("neg_max", [P, S_STEP])
        row_sum = sb("row_sum", [P, 4, 4])
        inv_sum = sb("inv_sum", [P, 4, 4])
        o_t = sb("o_t", [P, 2, 512])
        xn = roped[:, :, :].rearrange("p t (a d) -> p (t a) d", a=2)

        s_ps = ps("s_ps", [P, 2, 1024])
        o_ps = ps("o_ps", [P, 512])
        ring_ps = ps("ring_ps", [P, RING, 512])
        m_ps = ring_ps[:, 0, :]

        load_x = sem("load_x")
        load_c = sem("load_c")
        load_w = sem("load_w")
        load_o = sem("load_o")
        const_ready = sem("const_ready")
        ln_step = sem("ln_step")
        sd_ready = sem("sd_ready")
        xn_ready = sem("xn_ready")
        xn_turned = sem("xn_turned")
        xnT_ready = sem("xnT_ready")
        proj_done = sem("proj_done")
        qkv_ready = sem("qkv_ready")
        rope_part = sem("rope_part")
        rope_ready = sem("rope_ready")
        turned = sem("turned")
        qk_hi_ready = sem("qk_hi_ready")
        qk_ready = sem("qk_ready")
        spread = [sem(f"spread_half{hf}") for hf in range(2)]
        v_hi_ready = sem("v_hi_ready")
        v_ready = sem("v_ready")
        scores_ready = sem("scores_ready")
        max_ready = sem("max_ready")
        probs_ready = sem("probs_ready")
        pt_ready = sem("pt_ready")
        pt_hi_ready = sem("pt_hi_ready")
        pt_split = sem("pt_split")
        pv_done = sem("pv_done")
        o_ready = sem("o_ready")
        y_done = sem("y_done")
        inv_ready = sem("inv_ready")
        y_added = sem("y_added")
        gate_done = sem("gate_done")
        gate_step = sem("gate_step")
        gate_exp = sem("gate_exp")
        gate_shift = sem("gate_shift")
        count_part = sem("count_part")
        count_done = sem("count_done")
        flag_ready = sem("flag_ready")
        stored = sem("stored")
        fw_load = sem("fw_load")
        f_h = sem("f_h")
        f_z = sem("f_z")
        f_e = sem("f_e")
        f_act = sem("f_act")
        f_step = sem("f_step")
        f_y = sem("f_y")
        f_we = sem("f_we")
        f_add = sem("f_add")
        f_end = sem("f_end")

        lg = p0[:, 0:128].rearrange("p (t e) -> p t e", e=E)
        ex = p0[:, 128:256].rearrange("p (t e) -> p t e", e=E)
        pr = p0[:, 256:384].rearrange("p (t e) -> p t e", e=E)
        sel = p0[:, 384:512].rearrange("p (t e) -> p t e", e=E)
        wt = p0[:, 512:640].rearrange("p (t e) -> p t e", e=E)
        g_max = p0[:, 640:656]
        g_sum = p0[:, 656:672]
        g_inv = p0[:, 672:688]
        cnt = p0[:, 688:696]
        keep = p0[:, 696:704]
        any_kept = p0[:, 704:705]
        we = p0[:, 720:736]
        b1c = p0[:, 740:741]
        b2r = p0[0:1, 768:896]
        gt = p1[:, 0:1024].rearrange("p (t e j) -> p t e j", e=E, j=E)
        eq = p1[:, 1024:2048].rearrange("p (t e j) -> p t e j", e=E, j=E)
        z_s = p1[:, 2048:2560]
        e_s = p1[:, 2560:3072]
        w1_s = qkv[:, 0, 0:128]
        w2_s = qkv[:, 0, 128:256]
        hs = o_t[:, 0, :]
        flag = sb("flag", [P, 1], I32)

        def p_off(c, j):
            return sum((4 * c + i + 1) * P for i in range(j))

        def pt_cols(c, ki):
            start = 0
            for k in range(ki + 1):
                first = max(0, k - 4 * c)
                pad = 1 if first == 3 else 0
                width = (4 - first + pad) * P
                if k == ki:
                    return start, width, (first - pad) * P, pad * P
                start += width

        probs = [p0, p1]
        pt_hi = [pt_hi0, pt_hi1]
        pt_lo = [pt_lo0, pt_lo1]
        block = ctx.enter_context(nc.Block())

        def bank(item):
            return ring_ps[:, BANK[item], :]

        def s_cols(u, j):
            wide = UNITS[u][1] == 1
            return s_ps[:, j % 2, :] if wide else s_ps[:, j % 2, 512 * (j // 2):512 * (j // 2) + 512]

        def at(per_step, p, b, i):
            return p * (2 * per_step) + (b * per_step + i)

        def run(eng, step):
            for b in range(B):
                step(0, b, b == 0, False)
            with eng.Fori(1, PAIRS - 1) as p:
                for b in range(B):
                    step(p, b, False, False)
            for b in range(B):
                step(PAIRS - 1, b, False, b == 1)

        def skipped(item, first, last):
            back = item[0] in ("PV", "Y") and item[1] == 1
            ahead = item[0] in ("J", "X") or (item[0] == "S" and item[1] == 1)
            return (first and back) or (last and ahead)

        @block.sync
        def _(sp):
            sp.dma_start(y[:, 0:QT, :], x_v[:, 0:QT, :]).then_inc(load_x, 16)
            sp.dma_start(y[:, QT:TILES, :], x_v[:, QT:TILES, :]).then_inc(load_x, 16)
            sp.dma_start(ident[:, :], ident_in).then_inc(load_c, 16)
            sp.dma_start(w_qkv[:, :], qkv_wT).then_inc(load_w, 16)
            sp.dma_start(cos_s[:, :, :], cos).then_inc(load_c, 16)
            sp.dma_start(sin_s[:, :, :], sin).then_inc(load_c, 16)
            sp.dma_start(mask_f[:, :], mask_in).then_inc(load_c, 16)
            sp.dma_start(lower[:, :, :], lower_in).then_inc(load_c, 16)
            sp.dma_start(w_out[0:64, :, :], out_wT).then_inc(load_o, 16)
            sp.dma_start(w_out[64:128, :, :], out_wT).then_inc(load_o, 16)
            sp.dma_start(w_gate[:, :], gate_wT).then_inc(load_o, 16)

            def spread_step(p, b):
                for hf in range(2):
                    cols = slice(512 * hf, 512 * hf + 512)
                    for k in range(2):
                        sp.wait_ge(qk_ready, at(X_STEP, p, b, 2 * hf + k + 1))
                        for h in range(2):
                            rows = slice(64 * h, 64 * h + 64)
                            for half in (slice(0, 64), slice(64, 128)):
                                if k:
                                    sp.dma_start(k_st[half, b, h, :, cols].bitcast(F32),
                                                 qk_pair[rows, hf, 1, :, :].bitcast(F32)).then_inc(spread[hf], 16)
                                else:
                                    sp.dma_start(q_st[half, b, h, cols].bitcast(F32),
                                                 qk_pair[rows, hf, 0, half.start // 64, :].bitcast(F32)).then_inc(spread[hf], 16)

            for b in range(B):
                spread_step(0, b)
            with sp.Fori(1, PAIRS) as p:
                for b in range(B):
                    spread_step(p, b)

            sp.wait_ge(y_added, 4 * STEPS)
            sp.dma_start(out_v, y[:, :, :]).then_inc(stored, 16)
            sp.wait_ge(stored, 16)
            sp.wait_ge(flag_ready, 1)
            kept = sp.value_load(flag[0:1, 0:1], min_val=0, max_val=1)
            with sp.If(kept):
                def load_expert(e):
                    sp.dma_start(w1_s, w1T[bass.ds(e, 1)].rearrange("a h f -> (a h) f")).then_inc(fw_load, 16)
                    sp.dma_start(w2_s, w2T[bass.ds(e, 1)].rearrange("a f g -> (a f) g")).then_inc(fw_load, 16)
                    sp.dma_start(b1c, b1T[bass.ds(e, 1)].rearrange("a f o -> (a f) o")).then_inc(fw_load, 16)
                    sp.dma_start(b2r, b2[bass.ds(e, 1)]).then_inc(fw_load, 16)

                load_expert(0)
                with sp.Fori(1, E) as e:
                    sp.wait_ge(f_add, e * 4)
                    load_expert(e)
                sp.wait_ge(f_add, 4 * E)
                sp.dma_start(out_v, y[:, :, :]).then_inc(stored, 16)
                sp.wait_ge(stored, 32)
            sp.nop()

        @block.gpsimd
        def _(pool):
            def rope(p, b, first):
                for hf in range(2):
                    t0 = 4 * hf
                    src = qkv[:, t0:t0 + 4, 0:256].rearrange("p t (s d) -> p t s d", d=64)
                    dst = roped[:, t0:t0 + 4, :].rearrange("p t (s d) -> p t s d", d=64)
                    by_sin = rope_sin[:, :, :].rearrange("p t (s d) -> p t s d", d=64)

                    def table(tab, lo, n):
                        return tab[:, t0:t0 + 4, lo:lo + n].unsqueeze(2).to_broadcast([P, 4, 4, n])

                    pool.wait_ge(qkv_ready, at(J_STEP, p, b, 4 * hf + 4))
                    if first:
                        pool.wait_ge(load_c, 16 * 5)
                        pool.wait_ge(xn_turned, 4)
                    else:
                        pool.wait_ge(turned, at(X_STEP, p, b - 1, 2 * hf + 2))
                    pool.tensor_tensor(dst, src, table(cos_s, 0, 64), ALU.mult).then_inc(rope_part, 1)
                    if hf or not first:
                        pool.wait_ge(rope_ready, at(2, p, b, hf))
                    pool.tensor_tensor(by_sin[:, :, :, 0:32], src[:, :, :, 32:64], table(sin_s, 0, 32),
                                       ALU.mult).then_inc(rope_part, 1)
                    pool.tensor_tensor(by_sin[:, :, :, 32:64], src[:, :, :, 0:32], table(sin_s, 32, 32),
                                       ALU.mult).then_inc(rope_part, 1)
                    pool.wait_ge(rope_part, at(6, p, b, 3 * hf + 3))
                    pool.tensor_tensor(dst, dst, by_sin, ALU.add).then_inc(rope_ready, 1)

            def values(p, b, reused):
                v = qkv[:, :, 256:384].rearrange("p t (h d) -> p t h d", d=64)
                if reused:
                    pool.wait_ge(pv_done, at(4, p, b - 2, 4))
                dst = v_st[:, b, :, :, :]
                pool.tensor_tensor(dst[:, :, :, 0:64], v, ones[:, 0:1].unsqueeze(2).unsqueeze(3).to_broadcast(
                    [P, QT, 2, 64]), ALU.mult).then_inc(v_hi_ready, 1)
                pool.wait_ge(v_hi_ready, at(1, p, b, 1))
                pool.tensor_tensor(dst[:, :, :, 64:128], v, dst[:, :, :, 0:64], ALU.subtract).then_inc(v_ready, 1)

            pool.wait_ge(const_ready, 7)
            for b in range(B):
                rope(0, b, b == 0)
                values(0, b, False)
            with pool.Fori(1, PAIRS) as p:
                for b in range(B):
                    rope(p, b, False)
                    values(p, b, True)

        @block.scalar
        def _(act):
            def deviation(n):
                act.wait_ge(ln_step, n)
                nc.scalar.activation(sd[:, :], ve[:, :], ACT.Sqrt).then_inc(sd_ready, 1)

            def xn_copy(n0):
                for g in range(4):
                    act.wait_ge(xn_turned, n0 + g + 1)
                    nc.scalar.activation(xnT[:, 512 * g:512 * g + 512], ring_ps[:, g % 2, :],
                                         ACT.Copy).then_inc(xnT_ready, 1)

            def project(p, b, t, first):
                if t == 0 and not first:
                    act.wait_ge(rope_ready, at(2, p, b, 0))
                    act.wait_ge(v_ready, at(1, p, b, 0))
                act.wait_ge(proj_done, at(J_STEP, p, b, t + 1))
                nc.scalar.activation(qkv[:, t, :], bank(("J", t))[:, 0:384], ACT.Copy).then_inc(qkv_ready, 1)

            def high(p, b, xi, first):
                hf, k = xi // 2, xi % 2
                if not first:
                    act.wait_ge(spread[hf], 16 * at(SPREADS, p, b, 0))
                act.wait_ge(turned, at(X_STEP, p, b, xi + 1))
                nc.scalar.activation(qk_pair[:, hf, k, 0, :], bank(("X", xi)), ACT.Copy,
                                     scale=1.0 if k else 0.125).then_inc(qk_hi_ready, 1)

            def exps(p, b, u, j, early):
                c = UNITS[u][1]
                w = (4 * c + j + 1) * P
                if j == 0 and not early:
                    act.wait_ge(pt_ready, at(T_STEP, p, b, [-8, 0, 4, 12][u]))
                act.wait_ge(max_ready, at(S_STEP, p, b, 4 * u + j + 1))
                o = p_off(c, j)
                nc.scalar.activation(probs[c][:, o:o + w], s_cols(u, j)[:, 0:w], ACT.Exp,
                                     bias=neg_max[:, 4 * u + j:4 * u + j + 1],
                                     accum_out=row_sum[:, u, j:j + 1]).then_inc(probs_ready, 1)

            def step(p, b, first, last):
                start = first or (isinstance(p, int) and p == 0)
                pend = []
                for item in ACT_ORDER:
                    if skipped(item, first, last):
                        continue
                    if item[0] == "T":
                        _, u, ki = item
                        c = UNITS[u][1]
                        if ki == 0 and not (first and u < 2):
                            act.wait_ge(pv_done, at(4, p, b, u - 1))
                        act.wait_ge(pt_ready, at(T_STEP, p, b, T_OF[u] + ki + 1))
                        o, w, _, pad = pt_cols(c, ki)
                        nc.scalar.activation(pt_hi[c][:, o + pad:o + w], bank(item)[:, 0:w - pad],
                                             ACT.Copy).then_inc(pt_hi_ready, 1)
                    elif item[0] == "PV":
                        _, d, u, ki = item
                        if ki == KT[u] - 1:
                            if not (first and d == 0 and u < 2):
                                act.wait_ge(y_done, at(4, p, b - d, u - 1))
                            act.wait_ge(pv_done, at(4, p, b - d, u + 1))
                            nc.scalar.activation(o_t[:, u % 2, :], o_ps[:, :], ACT.Copy).then_inc(o_ready, 1)
                    elif item[0] == "S":
                        _, d, u, j = item
                        exps(p, b + d, u, j, first and d == 0 and u < 2)
                    elif item[0] == "J":
                        project(p, b + 1, item[1], False)
                    elif item[0] == "X":
                        high(p, b + 1, item[1], False)

            deviation(1)
            xn_copy(0)
            for t in range(QT):
                project(0, 0, t, True)
            for xi in range(X_STEP):
                high(0, 0, xi, True)
            for j in range(4):
                exps(0, 0, 0, j, True)
            run(act, step)
            act.wait_ge(y_done, 4 * STEPS - 2)
            act.wait_ge(pv_done, 4 * STEPS)
            nc.scalar.activation(o_t[:, 1, :], o_ps[:, :], ACT.Copy).then_inc(o_ready, 1)

            deviation(2)
            xn_copy(4)
            act.wait_ge(gate_shift, 1)
            nc.scalar.activation(ex, lg, ACT.Exp).then_inc(gate_exp, 1)

            act.wait_ge(flag_ready, 1)
            kept = act.value_load(flag[0:1, 0:1], min_val=0, max_val=1)
            with act.If(kept):
                with act.Fori(0, E) as e:
                    act.wait_ge(fw_load, e * 64 + 64)
                    for g in range(4):
                        act.wait_ge(f_h, e * 4 + (g + 1))
                        nc.scalar.activation(z_s, o_ps[:, :], ACT.Identity, bias=b1c).then_inc(f_z, 1)
                        act.wait_ge(f_z, e * 4 + (g + 1))
                        nc.scalar.activation(e_s, z_s, ACT.Exp, scale=-1.0).then_inc(f_e, 1)
            act.nop()

        @block.vector
        def _(dve):
            def layernorm(k):
                for t in range(TILES):
                    nc.vector.bn_stats(stats[:, t, :], y[:, t, :]).then_inc(gate_step, 1)
                dve.wait_ge(gate_step, link[0] + TILES)
                for t in range(TILES):
                    nc.vector.bn_aggr(mean_var[:, t, :], stats[:, t, :]).then_inc(gate_step, 1)
                dve.wait_ge(gate_step, link[0] + 2 * TILES)
                link[0] += 2 * TILES
                nc.vector.tensor_scalar(ve[:, :], mean_var[:, :, 1], EPS, None, ALU.add).then_inc(ln_step, 1)
                dve.wait_ge(sd_ready, k)
                after(nc.vector.reciprocal(r0[:, :], sd[:, :]))
                after(nc.vector.tensor_tensor(r1[:, :], r0[:, :], r0[:, :], ALU.mult))
                after(nc.vector.tensor_tensor(r1[:, :], r1[:, :], ve[:, :], ALU.mult))
                after(nc.vector.tensor_scalar(r1[:, :], r1[:, :], -0.5, 1.5, ALU.mult, ALU.add))
                after(nc.vector.tensor_tensor(rstd[:, :], r0[:, :], r1[:, :], ALU.mult))
                for t in range(TILES):
                    ins = nc.vector.tensor_scalar(xn[:, t, :], y[:, t, :], mean_var[:, t, 0:1], rstd[:, t:t + 1],
                                                  ALU.subtract, ALU.mult)
                    ins.then_inc(xn_ready, 1)

            link = [0]

            def after(ins):
                ins.then_inc(gate_step, 1)
                link[0] += 1
                dve.wait_ge(gate_step, link[0])

            def low(p, b, xi):
                hf, k = xi // 2, xi % 2
                dve.wait_ge(qk_hi_ready, at(X_STEP, p, b, xi + 1))
                nc.vector.scalar_tensor_tensor(out=qk_pair[:, hf, k, 1, :], in0=bank(("X", xi)),
                                               scalar=1.0 if k else 0.125, in1=qk_pair[:, hf, k, 0, :],
                                               op0=ALU.mult, op1=ALU.subtract).then_inc(qk_ready, 1)

            def maxes(p, b, u, j):
                w = (4 * UNITS[u][1] + j + 1) * P
                dve.wait_ge(scores_ready, at(S_STEP, p, b, 4 * u + j + 1))
                nc.vector.tensor_reduce(neg_max[:, 4 * u + j:4 * u + j + 1], s_cols(u, j)[:, 0:w], AX.X, ALU.max,
                                        negate=True).then_inc(max_ready, 1)

            def add_y(p, b, u, item):
                c = UNITS[u][1]
                dve.wait_ge(probs_ready, at(S_STEP, p, b, 4 * u + 4))
                nc.vector.reciprocal(inv_sum[:, u, :], row_sum[:, u, :]).then_inc(inv_ready, 1)
                dve.wait_ge(inv_ready, at(4, p, b, u + 1))
                dve.wait_ge(y_done, at(4, p, b, u + 1))
                for j in range(4):
                    rows = y[:, QT * (b % 2) + 4 * c + j, :]
                    ins = nc.vector.scalar_tensor_tensor(out=rows, in0=bank(item)[:, j * P:(j + 1) * P],
                                                         scalar=inv_sum[:, u, j:j + 1], in1=rows,
                                                         op0=ALU.mult, op1=ALU.add)
                ins.then_inc(y_added, 1)

            def step(p, b, first, last):
                for item in ORDER:
                    if skipped(item, first, last):
                        continue
                    if item[0] == "T":
                        _, u, ki = item
                        c = UNITS[u][1]
                        o, w, _, pad = pt_cols(c, ki)
                        dve.wait_ge(pt_hi_ready, at(T_STEP, p, b, T_OF[u] + ki + 1))
                        nc.vector.tensor_tensor(pt_lo[c][:, o + pad:o + w], bank(item)[:, 0:w - pad],
                                                pt_hi[c][:, o + pad:o + w], ALU.subtract).then_inc(pt_split, 1)
                    elif item[0] == "S":
                        maxes(p, b + item[1], item[2], item[3])
                    elif item[0] == "Y":
                        if not (first and item[1] == 0 and item[2] == 0):
                            dve.wait_ge(y_added, at(4, p, b - item[1], item[2]))
                        add_y(p, b - item[1], item[2], item)
                    elif item[0] == "X":
                        low(p, b + 1, item[1])

            nc.vector.memset(ones[:, :], 1.0).then_inc(const_ready, 1)
            for t in (pt_hi0, pt_lo0, pt_hi1, pt_lo1):
                n = t.shape[1]
                nc.vector.memset(t[:, n - 256:n - 128].bitcast(F32), 0.0).then_inc(const_ready, 1)
            dve.wait_ge(load_c, 16 * 5)
            nc.vector.tensor_copy(mask[:, :], mask_f[:, :]).then_inc(const_ready, 1)
            nc.vector.tensor_copy(ident_b[:, :], ident[:, :]).then_inc(const_ready, 1)
            dve.wait_ge(load_x, 32)
            layernorm(1)
            for xi in range(X_STEP):
                low(0, 0, xi)
            for j in range(4):
                maxes(0, 0, 0, j)
            maxes(0, 0, 1, 0)
            run(dve, step)
            dve.wait_ge(y_added, 4 * STEPS - 1)
            add_y(PAIRS - 1, 1, 3, ("Y", 1, 3))

            dve.wait_ge(y_added, 4 * STEPS)
            layernorm(2)
            dve.wait_ge(gate_done, 1)
            logits = m_ps[:, 0:TILES * E].rearrange("p (t e) -> p t e", e=E)
            wide = [P, TILES, E]
            after(nc.vector.tensor_reduce(g_max, logits, AX.X, ALU.max))
            nc.vector.tensor_tensor(lg, logits, g_max.unsqueeze(2).to_broadcast(wide), ALU.subtract).then_inc(gate_shift, 1)
            dve.wait_ge(gate_exp, 1)
            after(nc.vector.tensor_reduce(g_sum, ex, AX.X, ALU.add))
            after(nc.vector.reciprocal(g_inv, g_sum))
            after(nc.vector.tensor_tensor(pr, ex, g_inv.unsqueeze(2).to_broadcast(wide), ALU.mult))
            other = pr.unsqueeze(2).to_broadcast([P, TILES, E, E])
            own = pr.unsqueeze(3).to_broadcast([P, TILES, E, E])
            nc.vector.tensor_tensor(gt, other, own, ALU.is_gt).then_inc(gate_step, 1)
            link[0] += 1
            after(nc.vector.tensor_tensor(eq, other, own, ALU.is_equal))
            after(nc.vector.tensor_tensor(eq, eq, lower[:, :, :].unsqueeze(1).to_broadcast([P, TILES, E, E]), ALU.mult))
            after(nc.vector.tensor_tensor(gt, gt, eq, ALU.add))
            after(nc.vector.tensor_reduce(sel, gt, AX.X, ALU.add))
            after(nc.vector.tensor_scalar(sel, sel, 2.0, None, ALU.is_lt))
            nc.vector.tensor_reduce(cnt, sel.rearrange("p t e -> p e t"), AX.X, ALU.add).then_inc(count_part, 1)
            dve.wait_ge(count_done, 1)
            after(nc.vector.tensor_scalar(keep, m_ps[:, 256:256 + E], float(CAP), None, ALU.is_le))
            after(nc.vector.tensor_reduce(any_kept, keep, AX.X, ALU.max))
            nc.vector.tensor_copy(flag[:, :], any_kept).then_inc(flag_ready, 1)
            dve.wait_ge(flag_ready, 1)
            kept = dve.value_load(flag[0:1, 0:1], min_val=0, max_val=1)
            with dve.If(kept):
                after(nc.vector.tensor_tensor(sel, sel, keep.unsqueeze(1).to_broadcast(wide), ALU.mult))
                after(nc.vector.tensor_tensor(wt, pr, sel, ALU.mult))
                with dve.Fori(0, E) as e:
                    nc.vector.tensor_copy(we.unsqueeze(2), wt[:, :, bass.ds(e, 1)]).then_inc(f_we, 1)
                    for g in range(4):
                        dve.wait_ge(f_e, e * 4 + (g + 1))
                        nc.vector.tensor_scalar(e_s, e_s, 1.0, None, ALU.add).then_inc(f_step, 1)
                        dve.wait_ge(f_step, e * 8 + (2 * g + 1))
                        nc.vector.reciprocal(e_s, e_s).then_inc(f_step, 1)
                        dve.wait_ge(f_step, e * 8 + (2 * g + 2))
                        nc.vector.tensor_tensor(hs, z_s, e_s, ALU.mult).then_inc(f_act, 1)
                        dve.wait_ge(f_we, e + 1)
                        dve.wait_ge(f_y, e * 4 + (g + 1))
                        for j in range(4):
                            rows = y[:, 4 * g + j, :]
                            ins = nc.vector.scalar_tensor_tensor(out=rows, in0=m_ps[:, j * P:(j + 1) * P],
                                                                 scalar=we[:, 4 * g + j:4 * g + j + 1], in1=rows,
                                                                 op0=ALU.mult, op1=ALU.add)
                        ins.then_inc(f_add, 1)
                        dve.wait_ge(f_add, e * 4 + (g + 1))
            dve.nop()

        @block.tensor
        def _(pe):
            def turn_xn(n0):
                for g in range(4):
                    pe.wait_ge(xn_ready, n0 + 4 * g + 4)
                    if g >= 2:
                        pe.wait_ge(xnT_ready, n0 // 4 + g - 1)
                    for t in range(4):
                        mm = nc.tensor.transpose(ring_ps[:, g % 2, t * P:(t + 1) * P], xn[:, 4 * g + t, :], ident[:, :])
                    mm.then_inc(xn_turned, 1)

            def taken(p, b, item):
                if item[0] == "T":
                    pe.wait_ge(pt_split, at(T_STEP, p, b, T_OF[item[1]] + item[2] + 1))
                elif item[0] == "J":
                    pe.wait_ge(qkv_ready, at(J_STEP, p, b, item[1] + 1))
                elif item[0] == "X":
                    pe.wait_ge(qk_ready, at(X_STEP, p, b, item[1] + 1))
                else:
                    pe.wait_ge(y_added, at(4, p, b, item[2] + 1))

            def bank_free(p, b, item, first, last):
                before = bank_before(item, first, last)
                if before is None:
                    pe.wait_ge(qk_ready, X_STEP)
                    return
                was, back = before
                own = {"T": 0, "J": 1, "X": 1, "Y": -was[1] if was[0] == "Y" else 0}[was[0]]
                taken(p, b - back + own, was)

            def project(p, b, t):
                w = w_qkv[:, bass.ds(p * 384, 384)] if b < 2 else w_qkv[:, bass.ds(p * 384 + 384, 384)]
                col = (QT * (b % 2) + t) * P
                nc.tensor.matmul(bank(("J", t))[:, 0:384], xnT[:, col:col + P], w, start=True, stop=True).then_inc(proj_done, 1)

            def turn(p, b, xi):
                hf, k = xi // 2, xi % 2
                pe.wait_ge(rope_ready, at(2, p, b, hf + 1))
                for t in range(4):
                    src = roped[:, 4 * hf + t, k * P:(k + 1) * P]
                    mm = nc.tensor.transpose(bank(("X", xi))[:, t * P:(t + 1) * P], src, ident[:, :])
                mm.then_inc(turned, 1)

            def scores(p, b, u, j, early):
                h, c = UNITS[u]
                qt = 4 * c + j
                width = (qt + 2) // 2 * 2 * P
                if not early:
                    back = 4 if c == 0 and j >= 2 else 2
                    pe.wait_ge(probs_ready, at(S_STEP, p, b, 4 * u + j + 1 - back))
                if j == 0:
                    pe.wait_ge(spread[c], 16 * at(SPREADS, p, b, SPREADS))
                q = q_st[:, b % 2, h, qt * P:(qt + 1) * P]
                for lo in range(0, width, 512):
                    hi = min(lo + 512, width)
                    diag = lo <= qt * P < hi
                    o = s_cols(u, j)[:, lo:hi]
                    nc.tensor.matmul(o, q, k_st[:, b % 2, h, 0, lo:hi], start=True, stop=False)
                    mm = nc.tensor.matmul(o, q, k_st[:, b % 2, h, 1, lo:hi], start=False, stop=not diag)
                mm = nc.tensor.matmul(s_cols(u, j)[:, qt * P:(qt + 1) * P], ident_b[:, :], mask[:, :],
                                      start=False, stop=True)
                mm.then_inc(scores_ready, 1)

            def values(p, b, u, ki):
                h, c = UNITS[u]
                pe.wait_ge(pt_split, at(T_STEP, p, b, T_OF[u] + ki + 1))
                o, w, first_col, _ = pt_cols(c, ki)
                v = v_st[:, b % 2, ki, h, :]
                last = ki == KT[u] - 1
                nc.tensor.matmul(o_ps[:, first_col:512], v, pt_hi[c][:, o:o + w], start=(ki == 0), stop=False)
                mm = nc.tensor.matmul(o_ps[:, first_col:512], v, pt_lo[c][:, o:o + w], start=False, stop=last)
                if last:
                    mm.then_inc(pv_done, 1)

            def output(p, b, u, item):
                h = UNITS[u][0]
                pe.wait_ge(o_ready, at(4, p, b, u + 1))
                head = p * 2 + h if b >= 0 else p * 2 + (h - 2)
                w = w_out[:, bass.ds(head, 1), :].rearrange("p a d -> p (a d)")
                for j in range(4):
                    mm = nc.tensor.matmul(bank(item)[:, j * P:(j + 1) * P], o_t[:, u % 2, j * P:(j + 1) * P], w,
                                          start=True, stop=True)
                mm.then_inc(y_done, 1)

            def step(p, b, first, last):
                for item in ORDER:
                    if skipped(item, first, last):
                        continue
                    if item[0] in ("T", "J", "X", "Y"):
                        bank_free(p, b, item, first, last)
                    if item[0] == "T":
                        _, u, ki = item
                        c = UNITS[u][1]
                        if ki == 0:
                            pe.wait_ge(probs_ready, at(S_STEP, p, b, 4 * u + 4))
                        j0 = max(0, ki - 4 * c)
                        for j in range(j0, 4):
                            o = p_off(c, j) + ki * P
                            mm = nc.tensor.transpose(bank(item)[:, (j - j0) * P:(j - j0 + 1) * P],
                                                     probs[c][:, o:o + P], ident[:, :])
                        mm.then_inc(pt_ready, 1)
                    elif item[0] == "PV":
                        _, d, u, ki = item
                        if ki == 0:
                            if not (first and u == 0):
                                pe.wait_ge(o_ready, at(4, p, b, u))
                            if u == 0:
                                pe.wait_ge(v_ready, at(1, p, b, 1))
                        values(p, b - d, u, ki)
                    elif item[0] == "S":
                        scores(p, b + item[1], item[2], item[3], False)
                    elif item[0] == "J":
                        project(p, b + 1, item[1])
                    elif item[0] == "X":
                        turn(p, b + 1, item[1])
                    elif item[0] == "Y":
                        output(p, b - item[1], item[2], item)

            pe.wait_ge(load_c, 16 * 5)
            turn_xn(0)
            pe.wait_ge(xnT_ready, 4)
            pe.wait_ge(load_w, 16)
            pe.wait_ge(load_o, 48)
            pe.wait_ge(const_ready, 7)
            for t in range(QT):
                for was in range(t):
                    if BANK["J", was] == BANK["J", t]:
                        taken(0, 0, ("J", was))
                project(0, 0, t)
            taken(0, 0, ("J", QT - 1))
            for xi in range(X_STEP):
                for was in range(xi):
                    if BANK["X", was] == BANK["X", xi]:
                        taken(0, 0, ("X", was))
                turn(0, 0, xi)
            for j in range(4):
                scores(0, 0, 0, j, True)
            scores(0, 0, 1, 0, False)
            run(pe, step)
            for ki in range(8 - LAG, 8):
                values(PAIRS - 1, 1, 3, ki)
            pe.wait_ge(y_added, 4 * STEPS - 1)
            pe.wait_ge(pt_split, T_STEP * STEPS)
            output(PAIRS - 1, 1, 3, ("Y", 1, 3))

            pe.wait_ge(y_added, 4 * STEPS)
            turn_xn(TILES)
            pe.wait_ge(xnT_ready, 8)
            for t in range(TILES):
                mm = nc.tensor.matmul(m_ps[:, t * E:(t + 1) * E], xnT[:, t * P:(t + 1) * P], w_gate[:, :],
                                      start=True, stop=True)
            mm.then_inc(gate_done, 1)
            pe.wait_ge(count_part, 1)
            nc.tensor.matmul(m_ps[:, 256:256 + E], ones[:, :], cnt, start=True, stop=True).then_inc(count_done, 1)

            pe.wait_ge(flag_ready, 1)
            kept = pe.value_load(flag[0:1, 0:1], min_val=0, max_val=1)
            with pe.If(kept):
                with pe.Fori(0, E) as e:
                    pe.wait_ge(fw_load, e * 64 + 64)
                    for g in range(4):
                        nc.tensor.matmul(o_ps[:, :], w1_s, xnT[:, 512 * g:512 * g + 512],
                                         start=True, stop=True).then_inc(f_h, 1)
                        pe.wait_ge(f_act, e * 4 + (g + 1))
                        for j in range(4):
                            o = m_ps[:, j * P:(j + 1) * P]
                            nc.tensor.matmul(o, hs[:, j * P:(j + 1) * P], w2_s, start=True, stop=False)
                            mm = nc.tensor.matmul(o, ones[0:1, :], b2r, start=False, stop=True)
                        mm.then_inc(f_y, 1)
                        pe.wait_ge(f_add, e * 4 + (g + 1))
            pe.nop()


def kernel(L0_attn_x, L0_attn_qkv_w, L0_attn_out_w, L0_ffn_gate_w, L0_ffn_w1, L0_ffn_b1, L0_ffn_w2, L0_ffn_b2):
    import numpy as np
    import concourse.bacc as bacc
    from concourse.bass_utils import run_bass_kernel_spmd

    f32 = np.float32
    nb, T, D = L0_attn_x.shape
    N = nb * T
    E = L0_ffn_gate_w.shape[0]
    HD = L0_attn_out_w.shape[1]
    DH = 64
    pairs = HD // 128
    c = np.ascontiguousarray

    inv_freq = (f32(1.0) / np.power(f32(10000.0), np.arange(0, DH, 2, dtype=f32) / f32(DH))).astype(f32)
    freqs = np.arange(T, dtype=f32)[:, None] * inv_freq[None, :]
    cosv, sinv = np.cos(freqs).astype(f32), np.sin(freqs).astype(f32)
    cos = np.concatenate([cosv, cosv], 1).reshape(T // 128, 128, DH).transpose(1, 0, 2)
    sin = np.concatenate([-sinv, sinv], 1).reshape(T // 128, 128, DH).transpose(1, 0, 2)

    arrays = {
        "x": c(np.asarray(L0_attn_x).reshape(N, D)),
        "qkv_wT": c(np.asarray(L0_attn_qkv_w).reshape(3, pairs, 128, D).transpose(3, 1, 0, 2).reshape(D, 3 * HD)),
        "out_wT": c(np.asarray(L0_attn_out_w).reshape(D, HD // DH, DH).transpose(2, 1, 0)),
        "gate_wT": c(np.asarray(L0_ffn_gate_w).T),
        "w1T": c(np.asarray(L0_ffn_w1).transpose(0, 2, 1)),
        "b1T": c(np.asarray(L0_ffn_b1).reshape(E, D, 1)),
        "w2T": c(np.asarray(L0_ffn_w2).transpose(0, 2, 1)),
        "b2": c(np.asarray(L0_ffn_b2)),
        "cos": c(cos),
        "sin": c(sin),
        "ident_in": np.eye(128, dtype=f32),
        "mask_in": np.triu(np.full((128, 128), MASKED, dtype=f32), 1),
        "lower_in": c(np.broadcast_to(np.tril(np.ones((E, E), dtype=f32), -1), (128, E, E))),
    }
    nc = bacc.Bacc("TRN2", target_bir_lowering=False, num_devices=1)
    args = [nc.dram_tensor(f"in_{k}", a.shape, mybir.dt.from_np(a.dtype), kind="ExternalInput").ap()
            for k, a in arrays.items()]
    out = nc.dram_tensor("out_y", (N, D), F32, kind="ExternalOutput").ap()
    attention_moe_kernel(nc, *args, out)
    r = run_bass_kernel_spmd(nc, [{f"in_{k}": a for k, a in arrays.items()}], core_ids=[0])
    return r.results[0]["out_y"].reshape(nb, T, D)
```

```python
from contextlib import ExitStack

import concourse.bass as bass
from concourse import mybir

F32 = mybir.dt.float32
F32R = mybir.dt.float32r
BF16 = mybir.dt.bfloat16
I32 = mybir.dt.int32
ALU = mybir.AluOpType
ACT = mybir.ActivationFunctionType
AX = mybir.AxisListType

P = 128
MASKED = -3.0e38
EPS = 1e-5

UNITS = [(0, 0), (0, 1), (1, 0), (1, 1)]
KT = [4, 8, 4, 8]
T_OF = [0, 4, 12, 16]
T_STEP = 24
LAG = 3
S_STEP = 16
SPREADS = 4
SWAPS = 4
J_STEP = 4


def items(text):
    return [(i.rstrip("0123456789"), *(int(n) for n in i.lstrip("PVTSYJX"))) for i in text.split()]


ORDER = items("""
    J0 J1 S011  T00 S012  T01 PV135 PV136 PV137  T02 S013 J2 Y13 J3  T03 S020 PV000 PV001  T10 S021  T11
    T12 PV002 PV003 S022 S023  T13  T14 PV010  T15 PV011 S030  T16 PV012 PV013  T17  T20 S031 PV014 V0
    T21 V1 S032  T22 PV015 PV016  T23 PV017 S033 Y00 Y01 PV020 PV021 PV022 PV023 S100  T30 S101
    T31 S102  T32 S103  T33  T34 PV030 PV031 PV032  T35 PV033  T36  T37 PV034 S110 Y02
""")
ACT_ORDER = items("""
    S010 J0 J1  T00 S011  T01  T02 PV137 S012 J2 S013 J3  T03  T10 S020  T11  T12 PV003 S021 S022  T13
    T14  T15 S023 X0  T16  T17  T20 S030 V0  T21 V1 S031  T22  T23 PV017 S032 X1 S033 PV023  T30
    T31 S100  T32 S101  T33  T34 S102  T35  T36  T37 S103
""")
DVE_ORDER = items("""
    S011  T00 S012  T01  T02 S013 Y13 S020  T03 S021  T10  T11 S022  T12 S023  T13  T14  T15 S030  T16
    T17  T20 S031 V0  T21 V1 S032  T22  T23 S033 Y00 Y01 S100 S101  T30  T31 S102  T32  T33  T34 S103
    T35  T36  T37 S110 Y02
""")


GATE = {
    ("J", 0): [], ("J", 1): [], ("J", 2): [], ("J", 3): [], ("V", 0): [("GT", 0)], ("V", 1): [("GT", 1)],
    ("X", 0): [], ("X", 1): [], ("Y", 1, 3): [("Y", 1, 3), ("GN", 0)], ("Y", 0, 2): [("Y", 0, 2), ("GN", 1)],
    ("T", 3, 1): [("T", 3, 1), ("GL", 0), ("GS", 0)], ("T", 3, 2): [("T", 3, 2), ("GE", 0)],
}
STAND_IN = {("GT", 0): ("V", 0), ("GT", 1): ("V", 1)}


def with_gate(order):
    out = []
    for item in order:
        out += GATE.get(item, [item])
    return out


RING = 3
SHARED = [i for i in ORDER if i[0] in ("T", "J", "V", "Y")]
BANK = dict(zip(SHARED, (int(n) for n in "1212012012012012010210210210210210")))


def bank_before(item, first, last):
    item = STAND_IN.get(item, item)
    n, back = SHARED.index(item), 0
    while True:
        n -= 1
        if n < 0:
            if first:
                return None
            n, back = len(SHARED) - 1, 1
        was = SHARED[n]
        absent = (first and was[0] == "Y" and was[1] == 1) or (last and not back and GATE.get(was) == [])
        if BANK[was] == BANK[item] and not absent:
            return was, back


def attention_moe_kernel(nc, x, qkv_wT, out_wT, gate_wT, w1T, b1T, w2T, b2, cos, sin, ident_in, mask_in, lower_in, out):
    N, D = x.shape
    TILES = N // P
    B = 2
    QT = TILES // B
    E = gate_wT.shape[1]
    CAP = int(1.25 * N / E)
    PAIRS = qkv_wT.shape[1] // 384
    HALF = N // B // 2
    STEPS = 2 * PAIRS

    x_v = x.rearrange("(t p) d -> p t d", p=P)
    out_v = out.rearrange("(t p) d -> p t d", p=P)

    with ExitStack() as ctx:
        def sb(name, shape, dt=F32):
            return ctx.enter_context(nc.sbuf_tensor(name, shape, dt))

        def ps(name, shape, dt=F32):
            return ctx.enter_context(nc.psum_tensor(name, shape, dt))

        def sem(name):
            return ctx.enter_context(nc.semaphore(name))

        y = sb("y", [P, TILES, D])
        w_qkv = sb("w_qkv", [P, 384])
        w_out = sb("w_out", [P, 2, D])
        w_gate = sb("w_gate", [P, E])
        cos_s = sb("cos_s", [P, 2, HALF])
        sin_s = sb("sin_s", [P, 2, HALF])
        ident = sb("ident", [P, P])
        mask = sb("mask", [P, P], BF16)
        ident_b = sb("ident_b", [P, P], BF16)
        lower = sb("lower", [P, E, E])
        ones = sb("ones", [P, P])
        stats = sb("stats", [P, TILES, 6])
        mean_var = sb("mean_var", [P, TILES, 2])
        ve = sb("ve", [P, TILES])
        r0 = sb("r0", [P, TILES])
        r1 = sb("r1", [P, TILES])
        rstd = sb("rstd", [P, TILES])
        xnT = sb("xnT", [P, N])
        xnT_hi = sb("xnT_hi", [P, N], F32R)
        xnT_lo = sb("xnT_lo", [P, N], F32R)
        w_hi = sb("w_hi", [P, 2 * P], F32R)
        w_lo = sb("w_lo", [P, 2 * P], F32R)
        qk = sb("qk", [P, 2, 2, HALF])
        qk_swap = sb("qk_swap", [P, 2, 2, HALF])
        qk_pair = sb("qk_pair", [P, 2, 2, 2, 512], F32R)
        q_st = sb("q_st", [P, 2, 2, 1024], F32R)
        k_st = sb("k_st", [P, 2, 2, 2, 1024], F32R)
        v_st = sb("v_st", [P, 2, QT, 2, P], F32R)
        p0 = sb("p0", [P, 1280])
        p1 = sb("p1", [P, 3328])
        pt_hi0 = sb("pt_hi0", [P, 1408], F32R)
        pt_lo0 = sb("pt_lo0", [P, 1408], F32R)
        pt_hi1 = sb("pt_hi1", [P, 3456], F32R)
        pt_lo1 = sb("pt_lo1", [P, 3456], F32R)
        mask_f = p1[:, 2048:2048 + P]
        neg_max = sb("neg_max", [P, S_STEP])
        row_sum = sb("row_sum", [P, 4, 4])
        inv_sum = sb("inv_sum", [P, 4, 4])
        o_t = sb("o_t", [P, 2, 512])
        consts = sb("consts", [P, 2])
        xn_at = [p1[:, 0:2048].rearrange("p (t d) -> p t d", d=D),
                 qk[:, :, :, :].rearrange("p f k (t d) -> p (f k t) d", d=D)]

        s_ps = ps("s_ps", [P, 2, 1024])
        o_ps = ps("o_ps", [P, 512])
        ring_ps = ps("ring_ps", [P, RING, 512])
        m_ps = ring_ps[:, 0, :]
        logits_ps = [o.rearrange("p (t e) -> p t e", e=E) for o in
                     (s_ps[:, 1, 512:512 + QT * E], s_ps[:, 1, 0:4 * E], s_ps[:, 0, 512:512 + 4 * E])]
        counts_ps = s_ps[:, 1, 512:512 + E]

        load_x = [sem(f"load_x{g}") for g in range(4)]
        load_i = sem("load_i")
        load_t = sem("load_t")
        load_c = sem("load_c")
        load_w = sem("load_w")
        load_o = sem("load_o")
        load_gate = sem("load_gate")
        const_ready = sem("const_ready")
        const_pool = sem("const_pool")
        ln_step = sem("ln_step")
        root_ready = sem("root_ready")
        pool_step = sem("pool_step")
        xn_pool = sem("xn_pool")
        xn_ready = sem("xn_ready")
        xn_turned = sem("xn_turned")
        xnT_ready = sem("xnT_ready")
        xn_hi_ready = sem("xn_hi_ready")
        xn_split = sem("xn_split")
        w_hi_ready = sem("w_hi_ready")
        w_split = sem("w_split")
        proj_done = sem("proj_done")
        qkv_ready = sem("qkv_ready")
        rope_part = sem("rope_part")
        rope_ready = sem("rope_ready")
        swapped = [sem(f"swapped_half{hf}") for hf in range(2)]
        v_done = sem("v_done")
        qk_hi_ready = sem("qk_hi_ready")
        qk_ready = sem("qk_ready")
        spread = [[sem(f"spread_half{hf}_head{h}") for h in range(2)] for hf in range(2)]
        v_hi_ready = sem("v_hi_ready")
        v_ready = sem("v_ready")
        scores_ready = sem("scores_ready")
        max_ready = sem("max_ready")
        probs_ready = sem("probs_ready")
        pt_ready = sem("pt_ready")
        pt_hi_ready = sem("pt_hi_ready")
        pt_split = sem("pt_split")
        pv_done = sem("pv_done")
        o_ready = sem("o_ready")
        y_done = sem("y_done")
        inv_ready = sem("inv_ready")
        y_added = sem("y_added")
        gate_done = sem("gate_done")
        gate_step = sem("gate_step")
        gate_exp = sem("gate_exp")
        gate_shift = sem("gate_shift")
        count_part = sem("count_part")
        count_done = sem("count_done")
        flag_ready = sem("flag_ready")
        stored = sem("stored")
        fw_load = sem("fw_load")
        f_h = sem("f_h")
        f_z = sem("f_z")
        f_e = sem("f_e")
        f_act = sem("f_act")
        f_step = sem("f_step")
        f_y = sem("f_y")
        f_we = sem("f_we")
        f_add = sem("f_add")

        swap_flat = qk_swap[:, :, :, :].rearrange("p f k n -> p (f k n)")
        spare = swap_flat[:, 2 * P:]

        def by_tile(n):
            return spare[:, n * TILES * E:(n + 1) * TILES * E].rearrange("p (t e) -> p t e", e=E)

        shifted, ex, pr, sel = [by_tile(n) for n in range(4)]
        g_max = sb("g_max", [P, TILES])
        g_sum = sb("g_sum", [P, TILES])
        g_inv = sb("g_inv", [P, TILES])
        gt, eq = [spare[:, 4 * TILES * E + n * QT * E * E:4 * TILES * E + (n + 1) * QT * E * E].rearrange(
            "p (t e f) -> p t e f", e=E, f=E) for n in range(2)]
        PARTS = [slice(0, 8), slice(8, 12), slice(12, 16)]
        cnt = p0[:, 688:696]
        keep = p0[:, 696:704]
        any_kept = p0[:, 704:705]
        we = p0[:, 720:736]
        wt = p0[:, 512:640].rearrange("p (t e) -> p t e", e=E)
        b1c = p0[:, 740:741]
        b2r = p0[0:1, 768:896]
        z_s = p1[:, 2048:2560]
        e_s = p1[:, 2560:3072]
        w1_s = swap_flat[:, 0:P]
        w2_s = swap_flat[:, P:2 * P]
        hs = o_t[:, 0, :]
        flag = sb("flag", [P, 1], I32)

        def p_off(c, j):
            return sum((4 * c + i + 1) * P for i in range(j))

        def pt_cols(c, ki):
            start = 0
            for k in range(ki + 1):
                first = max(0, k - 4 * c)
                pad = 1 if first == 3 else 0
                width = (4 - first + pad) * P
                if k == ki:
                    return start, width, (first - pad) * P, pad * P
                start += width

        probs = [p0, p1]
        pt_hi = [pt_hi0, pt_hi1]
        pt_lo = [pt_lo0, pt_lo1]
        block = ctx.enter_context(nc.Block())

        def bank(item):
            return ring_ps[:, BANK[item], :]

        def s_cols(u, j):
            wide = UNITS[u][1] == 1
            return s_ps[:, j % 2, :] if wide else s_ps[:, j % 2, 512 * (j // 2):512 * (j // 2) + 512]

        def at(per_step, p, b, i):
            return p * (2 * per_step) + (b * per_step + i)

        def run(eng, step):
            for b in range(B):
                step(0, b, b == 0, False)
            with eng.Fori(1, PAIRS - 1) as p:
                for b in range(B):
                    step(p, b, False, False)
            for b in range(B):
                step(PAIRS - 1, b, False, b == 1)

        def skipped(item, first, last):
            back = item[0] in ("PV", "Y") and item[1] == 1
            ahead = item[0] in ("J", "V", "X") or (item[0] == "S" and item[1] == 1)
            return (first and back) or (last and ahead)

        def rotary(tab, hf):
            return tab[:, hf, :].unsqueeze(1).to_broadcast([P, 2, HALF])

        def values_of(b, hf):
            v = v_st[:, b, 4 * hf:4 * hf + 4, :, :]
            return v[:, :, :, 0:64], v[:, :, :, 64:128]

        @block.sync
        def _(sp):
            def load_rows(g):
                sp.dma_start(y[:, 4 * g:4 * g + 4, :], x_v[:, 4 * g:4 * g + 4, :]).then_inc(load_x[g], 16)

            load_rows(0)
            sp.dma_start(w_qkv[:, :], qkv_wT[:, 0:384]).then_inc(load_w, 16)
            load_rows(1)
            load_rows(2)
            load_rows(3)

            def load_out(heads):
                for half in (slice(0, 64), slice(64, 128)):
                    sp.dma_start(w_out[half, :, :], out_wT[:, heads, :]).then_inc(load_o, 16)

            load_out(slice(0, 2))

            def swap(p, b):
                for hf in range(2):
                    sp.wait_ge(qkv_ready, at(J_STEP, p, b, 2 * hf + 2))
                    for lo in range(0, P, 64):
                        for a, z in ((lo, lo + 32), (lo + 32, lo)):
                            sp.dma_start(qk_swap[a:a + 32, hf, :, :], qk[z:z + 32, hf, :, :]).then_inc(swapped[hf], 16)

            def spread_step(p, b):
                for hf in range(2):
                    cols = slice(512 * hf, 512 * hf + 512)
                    sp.wait_ge(qk_ready, at(2, p, b, hf + 1))
                    for h in range(2):
                        rows = slice(64 * h, 64 * h + 64)
                        for k in range(2):
                            for half in (slice(0, 64), slice(64, 128)):
                                if k:
                                    sp.dma_start(k_st[half, b, h, :, cols].bitcast(F32),
                                                 qk_pair[rows, hf, 1, :, :].bitcast(F32)).then_inc(spread[hf][h], 16)
                                else:
                                    part = half.start // 64
                                    sp.dma_start(q_st[half, b, h, cols].bitcast(F32),
                                                 qk_pair[rows, hf, 0, part, :].bitcast(F32)).then_inc(spread[hf][h], 16)

            def pair(p, first, last):
                for b in range(B):
                    swap(p, b)
                    if b == 1 and not first:
                        sp.wait_ge(y_done, at(4, p, 0, 0))
                        load_out(bass.ds(p * 2, 2))
                    if b == 1 and not last:
                        sp.wait_ge(v_done, at(2, p, 1, 2))
                        sp.dma_start(w_qkv[:, :], qkv_wT[:, bass.ds(p * 384 + 384, 384)]).then_inc(load_w, 16)
                    spread_step(p, b)

            pair(0, True, False)
            with sp.Fori(1, PAIRS - 1) as p:
                pair(p, False, False)
            pair(PAIRS - 1, False, True)

            sp.wait_ge(y_added, 4 * STEPS)
            sp.dma_start(out_v, y[:, :, :]).then_inc(stored, 16)
            sp.wait_ge(stored, 16)
            sp.wait_ge(flag_ready, 1)
            kept = sp.value_load(flag[0:1, 0:1], min_val=0, max_val=1)
            with sp.If(kept):
                def load_expert(e):
                    sp.dma_start(w1_s, w1T[bass.ds(e, 1)].rearrange("a h f -> (a h) f")).then_inc(fw_load, 16)
                    sp.dma_start(w2_s, w2T[bass.ds(e, 1)].rearrange("a f g -> (a f) g")).then_inc(fw_load, 16)
                    sp.dma_start(b1c, b1T[bass.ds(e, 1)].rearrange("a f o -> (a f) o")).then_inc(fw_load, 16)
                    sp.dma_start(b2r, b2[bass.ds(e, 1)]).then_inc(fw_load, 16)

                load_expert(0)
                with sp.Fori(1, E) as e:
                    sp.wait_ge(f_add, e * 4)
                    load_expert(e)
                sp.wait_ge(f_add, 4 * E)
                sp.dma_start(out_v, y[:, :, :]).then_inc(stored, 16)
                sp.wait_ge(stored, 32)
            sp.nop()

        @block.gpsimd
        def _(pool):
            def linked(ins):
                ins.then_inc(pool_step, 1)
                chain[0] += 1
                pool.wait_ge(pool_step, chain[0])

            chain = [0]

            def root(n, cols):
                pool.wait_ge(ln_step, n)
                return pool.tensor_tensor(r0[:, cols], ve[:, cols], consts[:, 0:1].to_broadcast(
                    [P, cols.stop - cols.start]), ALU.pow)

            def normalize(n, first, last, again):
                cols = slice(4 * first, 4 * last + 4)
                T = cols.stop - cols.start
                r, v, q = r0[:, cols], ve[:, cols], r1[:, cols]
                linked(root(n, cols))
                linked(pool.tensor_tensor(q, r, r, ALU.mult))
                linked(pool.tensor_tensor(q, q, v, ALU.mult))
                linked(pool.tensor_tensor(q, q, consts[:, 0:1].to_broadcast([P, T]), ALU.mult))
                linked(pool.tensor_tensor(q, q, consts[:, 1:2].to_broadcast([P, T]), ALU.add))
                linked(pool.tensor_tensor(rstd[:, cols], r, q, ALU.mult))
                xn = xn_at[again][:, cols, :]
                linked(pool.tensor_tensor(xn, y[:, cols, :], mean_var[:, cols, 0:1].to_broadcast([P, T, D]),
                                          ALU.subtract))
                pool.tensor_tensor(xn, xn, rstd[:, cols].unsqueeze(2).to_broadcast([P, T, D]),
                                   ALU.mult).then_inc(xn_pool, 1)

            def rotate(p, b):
                def times(dst, tab, hf):
                    pool.tensor_tensor(dst[:, hf, :, :], dst[:, hf, :, :], rotary(tab, hf), ALU.mult).then_inc(rope_part, 1)

                def rest(hf):
                    pool.wait_ge(qk_hi_ready, at(2, p, b, hf + 1))
                    pool.tensor_tensor(qk_pair[:, hf, :, 1, :], qk[:, hf, :, :], qk_pair[:, hf, :, 0, :],
                                       ALU.subtract).then_inc(qk_ready, 1)

                for hf in range(2):
                    pool.wait_ge(swapped[hf], 16 * at(SWAPS, p, b, SWAPS))
                    times(qk, cos_s, hf)
                    if hf:
                        rest(0)
                    times(qk_swap, sin_s, hf)
                    pool.wait_ge(rope_part, at(4, p, b, 2 * hf + 2))
                    pool.tensor_tensor(qk[:, hf, :, :], qk[:, hf, :, :], qk_swap[:, hf, :, :],
                                       ALU.add).then_inc(rope_ready, 1)
                rest(1)

            def split_weights(p):
                pool.wait_ge(load_w, 16 * (p + 1))
                w = w_qkv[:, 0:2 * P]
                pool.tensor_tensor(w_hi[:, :], w, ones[:, 0:1].to_broadcast([P, 2 * P]), ALU.mult).then_inc(w_hi_ready, 1)
                pool.wait_ge(w_hi_ready, p + 1)
                pool.tensor_tensor(w_lo[:, :], w, w_hi[:, :], ALU.subtract).then_inc(w_split, 1)

            pool.memset(consts[:, 0:1], -0.5).then_inc(const_pool, 1)
            pool.memset(consts[:, 1:2], 1.5).then_inc(const_pool, 1)
            pool.wait_ge(const_pool, 2)
            pool.wait_ge(const_ready, 1)
            for g in range(2):
                root(g + 1, slice(4 * g, 4 * g + 4)).then_inc(root_ready, 1)
                if g == 0:
                    split_weights(0)
            normalize(3, 2, 3, False)
            rotate(0, 1)
            split_weights(1)
            with pool.Fori(1, PAIRS - 1) as p:
                for b in range(B):
                    rotate(p, b)
                split_weights(p + 1)
            for b in range(B):
                rotate(PAIRS - 1, b)
            normalize(4, 0, 1, True)
            normalize(5, 2, 2, True)
            root(6, slice(12, 16)).then_inc(root_ready, 1)

        @block.scalar
        def _(act):
            act.dma_start(ident[:, :], ident_in).then_inc(load_i, 16)
            act.dma_start(cos_s[:, :, :], cos).then_inc(load_t, 16)
            act.dma_start(sin_s[:, :, :], sin).then_inc(load_t, 16)
            act.dma_start(mask_f, mask_in).then_inc(load_c, 16)
            act.dma_start(lower[:, :, :], lower_in).then_inc(load_c, 16)
            act.dma_start(w_gate[:, :], gate_wT).then_inc(load_gate, 16)

            def xn_copy(g, bank_of_g, again):
                act.wait_ge(xn_turned, 4 * again + g + 1)
                if not again:
                    nc.scalar.activation(xnT_hi[:, 512 * g:512 * g + 512], bank_of_g, ACT.Copy).then_inc(xn_hi_ready, 1)
                nc.scalar.activation(xnT[:, 512 * g:512 * g + 512], bank_of_g, ACT.Copy).then_inc(xnT_ready, 1)

            def gate_exps(part):
                act.wait_ge(gate_shift, part + 1)
                nc.scalar.activation(ex[:, PARTS[part], :], shifted[:, PARTS[part], :], ACT.Exp).then_inc(gate_exp, 1)

            def project(p, b, x, first):
                hf, k = x // 2, x % 2
                if k == 0 and not first:
                    act.wait_ge(qk_ready, at(2, p, b, hf - 1))
                act.wait_ge(proj_done, at(J_STEP, p, b, x + 1))
                nc.scalar.activation(qk[:, hf, k, :], bank(("J", x)), ACT.Copy,
                                     scale=1.0 if k else 0.125).then_inc(qkv_ready, 1)

            def high(p, b, hf, first):
                if not first:
                    for h in range(2):
                        act.wait_ge(spread[hf][h], 16 * at(SPREADS, p, b, 0))
                act.wait_ge(rope_ready, at(2, p, b, hf + 1))
                nc.scalar.activation(qk_pair[:, hf, :, 0, :], qk[:, hf, :, :], ACT.Copy).then_inc(qk_hi_ready, 1)

            def values(p, b, hf, reused):
                if reused:
                    act.wait_ge(pv_done, at(4, p, b - 2, 4))
                act.wait_ge(v_done, at(2, p, b, hf + 1))
                v = bank(("V", hf)).rearrange("p (t h d) -> p t h d", t=4, h=2)
                nc.scalar.activation(values_of(b % 2, hf)[0], v, ACT.Copy).then_inc(v_hi_ready, 1)

            def exps(p, b, u, j, early):
                c = UNITS[u][1]
                w = (4 * c + j + 1) * P
                if j == 0 and not early:
                    act.wait_ge(pt_ready, at(T_STEP, p, b, [-8, 0, 4, 12][u]))
                act.wait_ge(max_ready, at(S_STEP, p, b, 4 * u + j + 1))
                o = p_off(c, j)
                nc.scalar.activation(probs[c][:, o:o + w], s_cols(u, j)[:, 0:w], ACT.Exp,
                                     bias=neg_max[:, 4 * u + j:4 * u + j + 1],
                                     accum_out=row_sum[:, u, j:j + 1]).then_inc(probs_ready, 1)

            def step(p, b, first, last):
                for item in with_gate(ACT_ORDER) if last else ACT_ORDER:
                    if skipped(item, first, last):
                        continue
                    if item[0] == "T":
                        _, u, ki = item
                        c = UNITS[u][1]
                        if ki == 0 and not (first and u < 2):
                            act.wait_ge(pv_done, at(4, p, b, u - 1))
                        act.wait_ge(pt_ready, at(T_STEP, p, b, T_OF[u] + ki + 1))
                        o, w, _, pad = pt_cols(c, ki)
                        nc.scalar.activation(pt_hi[c][:, o + pad:o + w], bank(item)[:, 0:w - pad],
                                             ACT.Copy).then_inc(pt_hi_ready, 1)
                    elif item[0] == "PV":
                        _, d, u, ki = item
                        if ki == KT[u] - 1:
                            if not (first and d == 0 and u < 2):
                                act.wait_ge(y_done, at(4, p, b - d, u - 1))
                            act.wait_ge(pv_done, at(4, p, b - d, u + 1))
                            nc.scalar.activation(o_t[:, u % 2, :], o_ps[:, :], ACT.Copy).then_inc(o_ready, 1)
                    elif item[0] == "S":
                        _, d, u, j = item
                        exps(p, b + d, u, j, first and d == 0 and u < 2)
                    elif item[0] == "J":
                        project(p, b + 1, item[1], False)
                    elif item[0] == "X":
                        high(p, b + 1, item[1], False)
                    elif item[0] == "V":
                        values(p, b + 1, item[1], not first)
                    elif item[0] == "GT":
                        xn_copy(item[1], bank(STAND_IN[item]), True)
                    elif item[0] == "GE":
                        gate_exps(item[1])

            xn_copy(0, s_ps[:, 0, 0:512], False)
            for x in range(2):
                project(0, 0, x, True)
            xn_copy(1, s_ps[:, 0, 512:1024], False)
            values(0, 0, 0, False)
            for x in range(2, 4):
                project(0, 0, x, True)
            high(0, 0, 0, True)
            values(0, 0, 1, False)
            high(0, 0, 1, True)
            for j in range(4):
                exps(0, 0, 0, j, True)
            for g in range(2, 4):
                xn_copy(g, ring_ps[:, g - 2, :], False)
            run(act, step)
            act.wait_ge(y_done, 4 * STEPS - 2)
            act.wait_ge(pv_done, 4 * STEPS)
            nc.scalar.activation(o_t[:, 1, :], o_ps[:, :], ACT.Copy).then_inc(o_ready, 1)
            xn_copy(2, s_ps[:, 0, 0:512], True)
            gate_exps(1)
            xn_copy(3, s_ps[:, 0, 0:512], True)
            gate_exps(2)

            act.wait_ge(flag_ready, 1)
            kept = act.value_load(flag[0:1, 0:1], min_val=0, max_val=1)
            with act.If(kept):
                with act.Fori(0, E) as e:
                    act.wait_ge(fw_load, e * 64 + 64)
                    for g in range(4):
                        act.wait_ge(f_h, e * 4 + (g + 1))
                        nc.scalar.activation(z_s, o_ps[:, :], ACT.Identity, bias=b1c).then_inc(f_z, 1)
                        act.wait_ge(f_z, e * 4 + (g + 1))
                        nc.scalar.activation(e_s, z_s, ACT.Exp, scale=-1.0).then_inc(f_e, 1)
            act.nop()

        @block.vector
        def _(dve):
            def moments(first, last):
                tiles = range(4 * first, 4 * last + 4)
                for dst, src, op in ((stats, y, nc.vector.bn_stats), (mean_var, stats, nc.vector.bn_aggr)):
                    for t in tiles:
                        ins = op(dst[:, t, :], src[:, t, :]).then_inc(gate_step, 1)
                    link[0] += len(tiles)
                    dve.wait_ge(gate_step, link[0])
                cols = slice(4 * first, 4 * last + 4)
                nc.vector.tensor_scalar(ve[:, cols], mean_var[:, cols, 1], EPS, None, ALU.add).then_inc(ln_step, 1)

            def layernorm(g, n, again):
                cols = slice(4 * g, 4 * g + 4)
                dve.wait_ge(root_ready, n)
                after(nc.vector.tensor_tensor(r1[:, cols], r0[:, cols], r0[:, cols], ALU.mult))
                after(nc.vector.tensor_tensor(r1[:, cols], r1[:, cols], ve[:, cols], ALU.mult))
                after(nc.vector.tensor_scalar(r1[:, cols], r1[:, cols], -0.5, 1.5, ALU.mult, ALU.add))
                after(nc.vector.tensor_tensor(rstd[:, cols], r0[:, cols], r1[:, cols], ALU.mult))
                for t in range(4 * g, 4 * g + 4):
                    ins = nc.vector.tensor_scalar(xn_at[again][:, t, :], y[:, t, :], mean_var[:, t, 0:1],
                                                  rstd[:, t:t + 1], ALU.subtract, ALU.mult)
                ins.then_inc(xn_ready, 1)

            def shift(part):
                cols = PARTS[part]
                wide = [P, cols.stop - cols.start, E]
                logits = logits_ps[part]
                dve.wait_ge(gate_done, part + 1)
                after(nc.vector.tensor_reduce(g_max[:, cols], logits, AX.X, ALU.max))
                nc.vector.tensor_tensor(shifted[:, cols, :], logits, g_max[:, cols].unsqueeze(2).to_broadcast(wide),
                                        ALU.subtract).then_inc(gate_shift, 1)

            def choose(part):
                cols = PARTS[part]
                T = cols.stop - cols.start
                wide, square = [P, T, E], [P, T, E, E]
                larger, equal = gt[:, 0:T, :, :], eq[:, 0:T, :, :]
                dve.wait_ge(gate_exp, part + 1)
                after(nc.vector.tensor_reduce(g_sum[:, cols], ex[:, cols, :], AX.X, ALU.add))
                after(nc.vector.reciprocal(g_inv[:, cols], g_sum[:, cols]))
                after(nc.vector.tensor_tensor(pr[:, cols, :], ex[:, cols, :],
                                              g_inv[:, cols].unsqueeze(2).to_broadcast(wide), ALU.mult))
                other = pr[:, cols, :].unsqueeze(2).to_broadcast(square)
                own = pr[:, cols, :].unsqueeze(3).to_broadcast(square)
                nc.vector.tensor_tensor(larger, other, own, ALU.is_gt).then_inc(gate_step, 1)
                link[0] += 1
                after(nc.vector.tensor_tensor(equal, other, own, ALU.is_equal))
                after(nc.vector.tensor_tensor(equal, equal, lower[:, :, :].unsqueeze(1).to_broadcast(square), ALU.mult))
                after(nc.vector.tensor_tensor(larger, larger, equal, ALU.add))
                after(nc.vector.tensor_reduce(sel[:, cols, :], larger, AX.X, ALU.add))
                after(nc.vector.tensor_scalar(sel[:, cols, :], sel[:, cols, :], 2.0, None, ALU.is_lt))

            link = [0]

            def after(ins):
                ins.then_inc(gate_step, 1)
                link[0] += 1
                dve.wait_ge(gate_step, link[0])

            def xn_rest(g, bank_of_g):
                dve.wait_ge(xn_hi_ready, g + 1)
                dve.wait_ge(xnT_ready, g + 1)
                cols = slice(512 * g, 512 * g + 512)
                nc.vector.tensor_tensor(xnT_lo[:, cols], bank_of_g, xnT_hi[:, cols], ALU.subtract).then_inc(xn_split, 1)

            def values_rest(p, b, hf):
                dve.wait_ge(v_hi_ready, at(2, p, b, hf + 1))
                v = bank(("V", hf)).rearrange("p (t h d) -> p t h d", t=4, h=2)
                hi, lo = values_of(b % 2, hf)
                nc.vector.tensor_tensor(lo, v, hi, ALU.subtract).then_inc(v_ready, 1)

            def maxes(p, b, u, j):
                w = (4 * UNITS[u][1] + j + 1) * P
                dve.wait_ge(scores_ready, at(S_STEP, p, b, 4 * u + j + 1))
                nc.vector.tensor_reduce(neg_max[:, 4 * u + j:4 * u + j + 1], s_cols(u, j)[:, 0:w], AX.X, ALU.max,
                                        negate=True).then_inc(max_ready, 1)

            def add_y(p, b, u, item):
                c = UNITS[u][1]
                dve.wait_ge(probs_ready, at(S_STEP, p, b, 4 * u + 4))
                nc.vector.reciprocal(inv_sum[:, u, :], row_sum[:, u, :]).then_inc(inv_ready, 1)
                dve.wait_ge(inv_ready, at(4, p, b, u + 1))
                dve.wait_ge(y_done, at(4, p, b, u + 1))
                for j in range(4):
                    rows = y[:, QT * (b % 2) + 4 * c + j, :]
                    ins = nc.vector.scalar_tensor_tensor(out=rows, in0=bank(item)[:, j * P:(j + 1) * P],
                                                         scalar=inv_sum[:, u, j:j + 1], in1=rows,
                                                         op0=ALU.mult, op1=ALU.add)
                ins.then_inc(y_added, 1)

            def step(p, b, first, last):
                for item in with_gate(DVE_ORDER) if last else DVE_ORDER:
                    if skipped(item, first, last):
                        continue
                    if item[0] == "T":
                        _, u, ki = item
                        c = UNITS[u][1]
                        o, w, _, pad = pt_cols(c, ki)
                        dve.wait_ge(pt_hi_ready, at(T_STEP, p, b, T_OF[u] + ki + 1))
                        nc.vector.tensor_tensor(pt_lo[c][:, o + pad:o + w], bank(item)[:, 0:w - pad],
                                                pt_hi[c][:, o + pad:o + w], ALU.subtract).then_inc(pt_split, 1)
                    elif item[0] == "S":
                        maxes(p, b + item[1], item[2], item[3])
                    elif item[0] == "Y":
                        if not (first and item[1] == 0 and item[2] == 0):
                            dve.wait_ge(y_added, at(4, p, b - item[1], item[2]))
                        add_y(p, b - item[1], item[2], item)
                    elif item[0] == "V":
                        values_rest(p, b + 1, item[1])
                    elif item[0] == "GN":
                        dve.wait_ge(y_added, 4 * STEPS - (1 if item[1] else 4))
                        moments(*((2, 2) if item[1] else (0, 1)))
                    elif item[0] == "GS":
                        shift(item[1])


            def rotate_first(hf):
                dve.wait_ge(swapped[hf], 16 * SWAPS)
                for dst, tab in ((qk, cos_s), (qk_swap, sin_s)):
                    nc.vector.tensor_tensor(dst[:, hf, :, :], dst[:, hf, :, :], rotary(tab, hf),
                                            ALU.mult).then_inc(rope_part, 1)
                dve.wait_ge(rope_part, 2 * hf + 2)
                nc.vector.tensor_tensor(qk[:, hf, :, :], qk[:, hf, :, :], qk_swap[:, hf, :, :],
                                        ALU.add).then_inc(rope_ready, 1)

            def rest_first(hf):
                dve.wait_ge(qk_hi_ready, hf + 1)
                nc.vector.tensor_tensor(qk_pair[:, hf, :, 1, :], qk[:, hf, :, :], qk_pair[:, hf, :, 0, :],
                                        ALU.subtract).then_inc(qk_ready, 1)

            nc.vector.memset(ones[:, :], 1.0).then_inc(const_ready, 1)
            for t in (pt_hi0, pt_lo0, pt_hi1, pt_lo1):
                n = t.shape[1]
                nc.vector.memset(t[:, n - 256:n - 128].bitcast(F32), 0.0).then_inc(const_ready, 1)
            dve.wait_ge(load_x[0], 16)
            moments(0, 0)
            layernorm(0, 1, False)
            dve.wait_ge(load_x[1], 16)
            moments(1, 1)
            xn_rest(0, s_ps[:, 0, 0:512])
            layernorm(1, 2, False)
            dve.wait_ge(load_i, 16)
            nc.vector.tensor_copy(ident_b[:, :], ident[:, :]).then_inc(const_ready, 1)
            dve.wait_ge(load_c, 32)
            nc.vector.tensor_copy(mask[:, :], mask_f).then_inc(const_ready, 1)
            for g in range(2, 4):
                dve.wait_ge(load_x[g], 16)
            moments(2, 3)
            dve.wait_ge(load_t, 32)
            xn_rest(1, s_ps[:, 0, 512:1024])
            values_rest(0, 0, 0)
            rotate_first(0)
            rest_first(0)
            rotate_first(1)
            values_rest(0, 0, 1)
            rest_first(1)
            for j in range(4):
                maxes(0, 0, 0, j)
            for g in range(2, 4):
                xn_rest(g, ring_ps[:, g - 2, :])
            maxes(0, 0, 1, 0)
            run(dve, step)
            choose(0)
            dve.wait_ge(y_added, 4 * STEPS - 1)
            add_y(PAIRS - 1, 1, 3, ("Y", 1, 3))

            dve.wait_ge(y_added, 4 * STEPS)
            moments(3, 3)
            layernorm(3, 3, True)
            shift(1)
            choose(1)
            shift(2)
            choose(2)
            nc.vector.tensor_reduce(cnt, sel[:, :, :].rearrange("p t e -> p e t"), AX.X, ALU.add).then_inc(count_part, 1)
            dve.wait_ge(count_done, 1)
            after(nc.vector.tensor_scalar(keep, counts_ps, float(CAP), None, ALU.is_le))
            after(nc.vector.tensor_reduce(any_kept, keep, AX.X, ALU.max))
            nc.vector.tensor_copy(flag[:, :], any_kept).then_inc(flag_ready, 1)
            dve.wait_ge(flag_ready, 1)
            kept = dve.value_load(flag[0:1, 0:1], min_val=0, max_val=1)
            with dve.If(kept):
                after(nc.vector.tensor_tensor(sel[:, :, :], sel[:, :, :], keep.unsqueeze(1).to_broadcast([P, TILES, E]),
                                              ALU.mult))
                after(nc.vector.tensor_tensor(wt, pr[:, :, :], sel[:, :, :], ALU.mult))
                with dve.Fori(0, E) as e:
                    nc.vector.tensor_copy(we.unsqueeze(2), wt[:, :, bass.ds(e, 1)]).then_inc(f_we, 1)
                    for g in range(4):
                        dve.wait_ge(f_e, e * 4 + (g + 1))
                        nc.vector.tensor_scalar(e_s, e_s, 1.0, None, ALU.add).then_inc(f_step, 1)
                        dve.wait_ge(f_step, e * 8 + (2 * g + 1))
                        nc.vector.reciprocal(e_s, e_s).then_inc(f_step, 1)
                        dve.wait_ge(f_step, e * 8 + (2 * g + 2))
                        nc.vector.tensor_tensor(hs, z_s, e_s, ALU.mult).then_inc(f_act, 1)
                        dve.wait_ge(f_we, e + 1)
                        dve.wait_ge(f_y, e * 4 + (g + 1))
                        for j in range(4):
                            rows = y[:, 4 * g + j, :]
                            ins = nc.vector.scalar_tensor_tensor(out=rows, in0=m_ps[:, j * P:(j + 1) * P],
                                                                 scalar=we[:, 4 * g + j:4 * g + j + 1], in1=rows,
                                                                 op0=ALU.mult, op1=ALU.add)
                        ins.then_inc(f_add, 1)
                        dve.wait_ge(f_add, e * 4 + (g + 1))
            dve.nop()

        @block.tensor
        def _(pe):
            def turn_xn(g, bank_of_g, again):
                if again:
                    pe.wait_ge(*((xn_pool, [2, 2, 3][g]) if g < 3 else (xn_ready, 3)))
                else:
                    pe.wait_ge(*((xn_ready, g + 1) if g < 2 else (xn_pool, 1)))
                for t in range(4):
                    mm = nc.tensor.transpose(bank_of_g[:, t * P:(t + 1) * P], xn_at[again][:, 4 * g + t, :], ident[:, :])
                mm.then_inc(xn_turned, 1)

            def gate_logits(part):
                pe.wait_ge(xnT_ready, 4 + PARTS[part].stop // 4)
                for n, t in enumerate(range(PARTS[part].start, PARTS[part].stop)):
                    mm = nc.tensor.matmul(logits_ps[part][:, n, :], xnT[:, t * P:(t + 1) * P], w_gate[:, :],
                                          start=True, stop=True)
                mm.then_inc(gate_done, 1)

            def taken(p, b, item):
                if item[0] == "T":
                    pe.wait_ge(pt_split, at(T_STEP, p, b, T_OF[item[1]] + item[2] + 1))
                elif item[0] == "J":
                    pe.wait_ge(qkv_ready, at(J_STEP, p, b, item[1] + 1))
                elif item[0] == "V":
                    pe.wait_ge(v_ready, at(2, p, b, item[1] + 1))
                else:
                    pe.wait_ge(y_added, at(4, p, b, item[2] + 1))

            def bank_free(p, b, item, first, last):
                before = bank_before(item, first, last)
                if before is None:
                    pe.wait_ge(xn_split, 4)
                    return
                was, back = before
                if last and not back and was in STAND_IN.values():
                    pe.wait_ge(xnT_ready, 4 + was[1] + 1)
                    return
                own = {"T": 0, "J": 1, "V": 1, "Y": -was[1] if was[0] == "Y" else 0}[was[0]]
                taken(p, b - back + own, was)

            def weights(p, b):
                pe.wait_ge(w_split, (p + b // 2) + 1)

            def project(p, b, x):
                hf, k = x // 2, x % 2
                if x == 0:
                    weights(p, b)
                col = (QT * (b % 2) + 4 * hf) * P
                o, rows, wk = bank(("J", x)), slice(col, col + HALF), slice(k * P, k * P + P)
                nc.tensor.matmul(o, w_hi[:, wk], xnT_hi[:, rows], start=True, stop=False)
                nc.tensor.matmul(o, w_hi[:, wk], xnT_lo[:, rows], start=False, stop=False)
                nc.tensor.matmul(o, w_lo[:, wk], xnT_hi[:, rows], start=False, stop=True).then_inc(proj_done, 1)

            def project_values(p, b, hf):
                for t in range(4):
                    col = (QT * (b % 2) + 4 * hf + t) * P
                    mm = nc.tensor.matmul(bank(("V", hf))[:, t * P:(t + 1) * P], xnT[:, col:col + P],
                                          w_qkv[:, 2 * P:3 * P], start=True, stop=True)
                mm.then_inc(v_done, 1)

            def scores(p, b, u, j, early):
                h, c = UNITS[u]
                qt = 4 * c + j
                width = (qt + 2) // 2 * 2 * P
                if not early:
                    back = 4 if c == 0 and j >= 2 else 2
                    pe.wait_ge(probs_ready, at(S_STEP, p, b, 4 * u + j + 1 - back))
                if j == 0:
                    pe.wait_ge(spread[c][h], 16 * at(SPREADS, p, b, SPREADS))
                q = q_st[:, b % 2, h, qt * P:(qt + 1) * P]
                for lo in range(0, width, 512):
                    hi = min(lo + 512, width)
                    diag = lo <= qt * P < hi
                    o = s_cols(u, j)[:, lo:hi]
                    nc.tensor.matmul(o, q, k_st[:, b % 2, h, 0, lo:hi], start=True, stop=False)
                    mm = nc.tensor.matmul(o, q, k_st[:, b % 2, h, 1, lo:hi], start=False, stop=not diag)
                mm = nc.tensor.matmul(s_cols(u, j)[:, qt * P:(qt + 1) * P], ident_b[:, :], mask[:, :],
                                      start=False, stop=True)
                mm.then_inc(scores_ready, 1)

            def values(p, b, u, ki):
                h, c = UNITS[u]
                pe.wait_ge(pt_split, at(T_STEP, p, b, T_OF[u] + ki + 1))
                o, w, first_col, _ = pt_cols(c, ki)
                v = v_st[:, b % 2, ki, h, :]
                last = ki == KT[u] - 1
                nc.tensor.matmul(o_ps[:, first_col:512], v, pt_hi[c][:, o:o + w], start=(ki == 0), stop=False)
                mm = nc.tensor.matmul(o_ps[:, first_col:512], v, pt_lo[c][:, o:o + w], start=False, stop=last)
                if last:
                    mm.then_inc(pv_done, 1)

            def output(p, b, u, item):
                h = UNITS[u][0]
                pe.wait_ge(o_ready, at(4, p, b, u + 1))
                if u == 0 and b % 2 == 0:
                    pe.wait_ge(load_o, p * 32 + 32)
                w = w_out[:, h, :]
                for j in range(4):
                    mm = nc.tensor.matmul(bank(item)[:, j * P:(j + 1) * P], o_t[:, u % 2, j * P:(j + 1) * P], w,
                                          start=True, stop=True)
                mm.then_inc(y_done, 1)

            def step(p, b, first, last):
                for item in with_gate(ORDER) if last else ORDER:
                    if skipped(item, first, last):
                        continue
                    if item[0] in ("T", "J", "V", "Y", "GT"):
                        bank_free(p, b, item, first, last)
                    if item[0] == "T":
                        _, u, ki = item
                        c = UNITS[u][1]
                        if ki == 0:
                            pe.wait_ge(probs_ready, at(S_STEP, p, b, 4 * u + 4))
                        j0 = max(0, ki - 4 * c)
                        for j in range(j0, 4):
                            o = p_off(c, j) + ki * P
                            mm = nc.tensor.transpose(bank(item)[:, (j - j0) * P:(j - j0 + 1) * P],
                                                     probs[c][:, o:o + P], ident[:, :])
                        mm.then_inc(pt_ready, 1)
                    elif item[0] == "PV":
                        _, d, u, ki = item
                        if ki == 0:
                            if not (first and u == 0):
                                pe.wait_ge(o_ready, at(4, p, b, u))
                            if u == 0:
                                pe.wait_ge(v_ready, at(2, p, b, 2))
                        values(p, b - d, u, ki)
                    elif item[0] == "S":
                        scores(p, b + item[1], item[2], item[3], False)
                    elif item[0] == "J":
                        project(p, b + 1, item[1])
                    elif item[0] == "V":
                        project_values(p, b + 1, item[1])
                    elif item[0] == "Y":
                        output(p, b - item[1], item[2], item)
                    elif item[0] == "GT":
                        turn_xn(item[1], bank(STAND_IN[item]), True)
                    elif item[0] == "GL":
                        gate_logits(item[1])

            pe.wait_ge(load_i, 16)
            filled = []

            def fill(item):
                for was in filled:
                    if BANK[was] == BANK[item]:
                        taken(0, 0, was)
                if item[0] == "J":
                    project(0, 0, item[1])
                else:
                    project_values(0, 0, item[1])
                filled.append(item)

            turn_xn(0, s_ps[:, 0, 0:512], False)
            pe.wait_ge(xn_split, 1)
            for x in range(2):
                fill(("J", x))
            turn_xn(1, s_ps[:, 0, 512:1024], False)
            fill(("V", 0))
            pe.wait_ge(xn_split, 2)
            for x in range(2, 4):
                fill(("J", x))
            fill(("V", 1))
            pe.wait_ge(load_gate, 16)
            pe.wait_ge(const_ready, 7)
            for j in range(4):
                scores(0, 0, 0, j, True)
            taken(0, 0, ("J", J_STEP - 1))
            taken(0, 0, ("V", 1))
            for g in range(2, 4):
                turn_xn(g, ring_ps[:, g - 2, :], False)
            scores(0, 0, 1, 0, False)
            run(pe, step)
            for ki in range(8 - LAG, 8):
                values(PAIRS - 1, 1, 3, ki)
            pe.wait_ge(y_added, 4 * STEPS - 1)
            pe.wait_ge(pt_split, T_STEP * STEPS)
            output(PAIRS - 1, 1, 3, ("Y", 1, 3))
            for g in range(2, 4):
                turn_xn(g, s_ps[:, 0, 0:512], True)
                gate_logits(g - 1)
            pe.wait_ge(count_part, 1)
            nc.tensor.matmul(counts_ps, ones[:, :], cnt, start=True, stop=True).then_inc(count_done, 1)

            pe.wait_ge(flag_ready, 1)
            kept = pe.value_load(flag[0:1, 0:1], min_val=0, max_val=1)
            with pe.If(kept):
                with pe.Fori(0, E) as e:
                    pe.wait_ge(fw_load, e * 64 + 64)
                    for g in range(4):
                        nc.tensor.matmul(o_ps[:, :], w1_s, xnT[:, 512 * g:512 * g + 512],
                                         start=True, stop=True).then_inc(f_h, 1)
                        pe.wait_ge(f_act, e * 4 + (g + 1))
                        for j in range(4):
                            o = m_ps[:, j * P:(j + 1) * P]
                            nc.tensor.matmul(o, hs[:, j * P:(j + 1) * P], w2_s, start=True, stop=False)
                            mm = nc.tensor.matmul(o, ones[0:1, :], b2r, start=False, stop=True)
                        mm.then_inc(f_y, 1)
                        pe.wait_ge(f_add, e * 4 + (g + 1))
            pe.nop()


def kernel(L0_attn_x, L0_attn_qkv_w, L0_attn_out_w, L0_ffn_gate_w, L0_ffn_w1, L0_ffn_b1, L0_ffn_w2, L0_ffn_b2):
    import numpy as np
    import concourse.bacc as bacc
    from concourse.bass_utils import run_bass_kernel_spmd

    f32 = np.float32
    nb, T, D = L0_attn_x.shape
    N = nb * T
    E = L0_ffn_gate_w.shape[0]
    HD = L0_attn_out_w.shape[1]
    DH = 64
    pairs = HD // 128
    c = np.ascontiguousarray

    inv_freq = (f32(1.0) / np.power(f32(10000.0), np.arange(0, DH, 2, dtype=f32) / f32(DH))).astype(f32)
    freqs = np.arange(T, dtype=f32)[:, None] * inv_freq[None, :]
    cosv, sinv = np.cos(freqs).astype(f32), np.sin(freqs).astype(f32)
    cos = np.concatenate([cosv, cosv, cosv, cosv], 1).T.reshape(128, 2, T // 2)
    sin = np.concatenate([-sinv, sinv, -sinv, sinv], 1).T.reshape(128, 2, T // 2)

    arrays = {
        "x": c(np.asarray(L0_attn_x).reshape(N, D)),
        "qkv_wT": c(np.asarray(L0_attn_qkv_w).reshape(3, pairs, 128, D).transpose(3, 1, 0, 2).reshape(D, 3 * HD)),
        "out_wT": c(np.asarray(L0_attn_out_w).reshape(D, HD // DH, DH).transpose(2, 1, 0)),
        "gate_wT": c(np.asarray(L0_ffn_gate_w).T),
        "w1T": c(np.asarray(L0_ffn_w1).transpose(0, 2, 1)),
        "b1T": c(np.asarray(L0_ffn_b1).reshape(E, D, 1)),
        "w2T": c(np.asarray(L0_ffn_w2).transpose(0, 2, 1)),
        "b2": c(np.asarray(L0_ffn_b2)),
        "cos": c(cos),
        "sin": c(sin),
        "ident_in": np.eye(128, dtype=f32),
        "mask_in": np.triu(np.full((128, 128), MASKED, dtype=f32), 1),
        "lower_in": c(np.broadcast_to(np.tril(np.ones((E, E), dtype=f32), -1), (128, E, E))),
    }
    nc = bacc.Bacc("TRN2", target_bir_lowering=False, num_devices=1)
    args = [nc.dram_tensor(f"in_{k}", a.shape, mybir.dt.from_np(a.dtype), kind="ExternalInput").ap()
            for k, a in arrays.items()]
    out = nc.dram_tensor("out_y", (N, D), F32, kind="ExternalOutput").ap()
    attention_moe_kernel(nc, *args, out)
    r = run_bass_kernel_spmd(nc, [{f"in_{k}": a for k, a in arrays.items()}], core_ids=[0])
    return r.results[0]["out_y"].reshape(nb, T, D)
```
